# Optimizing a Trainium2 kernel written in Bass

```python
import numpy as np
import jax
import jax.numpy as jnp

def _softmax(x, axis=-1):
    return jax.nn.softmax(x, axis=axis)

def _gelu(x):
    return jax.nn.gelu(x, approximate=True)

def _silu(x):
    return jax.nn.silu(x)

def _sigmoid(x):
    return jax.nn.sigmoid(x)

def _layernorm(x, axis=-1, eps=1e-05):
    m = jnp.mean(x, axis=axis, keepdims=True)
    v = jnp.var(x, axis=axis, keepdims=True)
    return (x - m) / jnp.sqrt(v + eps)

def _scatter_add(tgt, idx, src, axis=0):
    return tgt.at[idx].add(src)

def _segment_sum(src, seg, n):
    return jax.ops.segment_sum(src, seg, n)
kernel_name = 'mk_adj_resnorm_d2_adj_r2_ee8432'

def setup_inputs(seed: int=0):
    np.random.seed(seed)
    _w = jnp.asarray

    def _rec_inputs():
        import jax
        import jax.numpy as jnp
        _gk = jax.random.key(seed)
        x = -0.0001538 + 1 * jax.random.normal(jax.random.fold_in(_gk, 1), (32, 256, 384), jnp.float32)
        _a = jax.random.bernoulli(jax.random.fold_in(_gk, 2), 0.015625, (32, 256, 256))
        _a = jnp.logical_or(_a, jnp.swapaxes(_a, -1, -2))
        _a = jnp.logical_or(_a, jnp.eye(256, dtype=bool))
        _af = _a.astype(jnp.float32)
        _af = _af * jax.random.uniform(jax.random.fold_in(_gk, 3), (32, 256, 256), jnp.float32, 0.05, 4.42607)
        adj = _af
        return (x, adj)
    x, adj = _rec_inputs()

    def _L0_gnn_setup():
        import jax, jax.numpy as jnp
        import numpy as np
        NUM_HEADS = 12
        HIDDEN = 384
        HEAD = HIDDEN // NUM_HEADS
        B, N = (16, 256)
        key = jax.random.key(seed)
        ks = jax.random.split(key, 9)
        s = 0.02
        return {'x': jax.random.normal(ks[0], (B, N, HIDDEN), jnp.float32), 'spatial_encoding': jax.random.normal(ks[1], (B, N, N), jnp.float32), 'edge_encoding': jax.random.normal(ks[2], (B, N, N), jnp.float32), 'Wq': jax.random.normal(ks[3], (HIDDEN, HIDDEN), jnp.float32) * s, 'Wk': jax.random.normal(ks[4], (HIDDEN, HIDDEN), jnp.float32) * s, 'Wv': jax.random.normal(ks[5], (HIDDEN, HIDDEN), jnp.float32) * s, 'bv': jax.random.normal(ks[6], (HIDDEN,), jnp.float32) * s, 'Wo': jax.random.normal(ks[7], (HIDDEN, HIDDEN), jnp.float32) * s, 'bo': jax.random.normal(ks[8], (HIDDEN,), jnp.float32) * s}
    _L0_gnn_all = _L0_gnn_setup()
    _L0_gnn_in = {k: v for k, v in _L0_gnn_all.items() if k in ('Wq', 'Wk', 'Wv', 'bv', 'Wo', 'bo')}
    del _L0_gnn_all

    def _L1_gnn_setup():
        import jax, jax.numpy as jnp
        import numpy as np
        B, S, H, L = (32, 256, 384, 2)

        def _layer_norm(z, a, b, eps=0.001):
            mu = jnp.mean(z, axis=-1, keepdims=True)
            sigma = jnp.std(z, axis=-1, keepdims=True, ddof=1)
            return (z - mu) / (sigma + eps) * a + b
        key = jax.random.key(seed)
        ks = jax.random.split(key, 6)
        hidden_state = jax.random.normal(ks[0], (B, S, H), dtype=jnp.float32)
        adjacency_matrix = (jax.random.uniform(ks[1], (B, S, S)) < 0.2).astype(jnp.float32)
        W_left = 0.05 * jax.random.normal(ks[2], (L, H, H), dtype=jnp.float32)
        W_right = 0.05 * jax.random.normal(ks[3], (L, H, H), dtype=jnp.float32)
        W_lin = 0.05 * jax.random.normal(ks[4], (L, H, H), dtype=jnp.float32)
        b_lin = jnp.zeros((L, H), dtype=jnp.float32)
        ln_a = jnp.ones((L, H), dtype=jnp.float32)
        ln_b = jnp.zeros((L, H), dtype=jnp.float32)
        return {'hidden_state': hidden_state, 'adjacency_matrix': adjacency_matrix, 'W_left': W_left, 'W_right': W_right, 'W_lin': W_lin, 'b_lin': b_lin, 'ln_a': ln_a, 'ln_b': ln_b}
    _L1_gnn_all = _L1_gnn_setup()
    _L1_gnn_in = {k: v for k, v in _L1_gnn_all.items() if k in ('W_left', 'W_right', 'W_lin', 'b_lin', 'ln_a', 'ln_b')}
    del _L1_gnn_all
    return {'x': x, 'adj': adj, 'L0_gnn_Wq': _L0_gnn_in['Wq'], 'L0_gnn_Wk': _L0_gnn_in['Wk'], 'L0_gnn_Wv': _L0_gnn_in['Wv'], 'L0_gnn_bv': _L0_gnn_in['bv'], 'L0_gnn_Wo': _L0_gnn_in['Wo'], 'L0_gnn_bo': _L0_gnn_in['bo'], 'L1_gnn_W_left': _L1_gnn_in['W_left'], 'L1_gnn_W_right': _L1_gnn_in['W_right'], 'L1_gnn_W_lin': _L1_gnn_in['W_lin'], 'L1_gnn_b_lin': _L1_gnn_in['b_lin'], 'L1_gnn_ln_a': _L1_gnn_in['ln_a'], 'L1_gnn_ln_b': _L1_gnn_in['ln_b']}

def reference(x, adj, L0_gnn_Wq, L0_gnn_Wk, L0_gnn_Wv, L0_gnn_bv, L0_gnn_Wo, L0_gnn_bo, L1_gnn_W_left, L1_gnn_W_right, L1_gnn_W_lin, L1_gnn_b_lin, L1_gnn_ln_a, L1_gnn_ln_b):
    import jax
    import jax.numpy as jnp

    def _L0_gnn_ref(x, spatial_encoding, edge_encoding, Wq, Wk, Wv, bv, Wo, bo):
        import jax, jax.numpy as jnp
        import numpy as np
        NUM_HEADS = 12
        HIDDEN = 384
        HEAD = HIDDEN // NUM_HEADS
        B, N = (16, 256)
        b, n, h = x.shape
        scale = jnp.asarray(HIDDEN, x.dtype) ** (-0.5)
        q = (x @ Wq.T).reshape(b, n, NUM_HEADS, HEAD)
        k = (x @ Wk.T).reshape(b, n, NUM_HEADS, HEAD)
        v = (x @ Wv.T + bv).reshape(b, n, NUM_HEADS, HEAD)
        bias = (spatial_encoding + edge_encoding)[:, None]
        scores = jnp.einsum('bqhd,bkhd->bhqk', q, k) * scale + bias
        row_nonzero = jnp.any(scores != 0, axis=-1, keepdims=True)
        scores = jnp.where(row_nonzero, scores, -jnp.inf)
        p = jax.nn.softmax(scores, axis=-1)
        p = jnp.nan_to_num(p)
        out = jnp.einsum('bhqk,bkhd->bqhd', p, v).reshape(b, n, h)
        return out @ Wo.T + bo

    def _L1_gnn_ref(hidden_state, adjacency_matrix, W_left, W_right, W_lin, b_lin, ln_a, ln_b):
        import jax, jax.numpy as jnp
        import numpy as np
        B, S, H, L = (32, 256, 384, 2)

        def _layer_norm(z, a, b, eps=0.001):
            mu = jnp.mean(z, axis=-1, keepdims=True)
            sigma = jnp.std(z, axis=-1, keepdims=True, ddof=1)
            return (z - mu) / (sigma + eps) * a + b
        temper = float(np.sqrt(H))
        adj = adjacency_matrix
        adj_tri = jnp.triu(adj, k=1)
        diag_mask = jnp.triu(adj, k=0) - adj_tri
        h = hidden_state
        for l in range(L):
            m_left = jnp.einsum('bsh,oh->bso', h, W_left[l])
            m_right = jnp.einsum('bsh,oh->bso', h, W_right[l])
            u_left = jnp.einsum('bih,bjh->bij', h, m_left) / temper
            u_right = jnp.einsum('bih,bjh->bij', h, m_right) / temper
            u = u_left * adj_tri + u_left * diag_mask + u_right * jnp.swapaxes(adj_tri, 1, 2)
            delta_exp_u = jnp.exp(u) * adj
            attention = delta_exp_u / (jnp.sum(delta_exp_u, axis=2, keepdims=True) + 1e-10)
            h_lin = jnp.einsum('bsh,oh->bso', h, W_lin[l]) + b_lin[l]
            ctx = jnp.matmul(attention, h_lin)
            h = jax.nn.relu(_layer_norm(ctx, ln_a[l], ln_b[l]))
        return h
    x = _layernorm(x + _L0_gnn_ref(x, adj, adj, L0_gnn_Wq, L0_gnn_Wk, L0_gnn_Wv, L0_gnn_bv, L0_gnn_Wo, L0_gnn_bo), axis=-1)
    x = _layernorm(x + _L1_gnn_ref(x, adj, L1_gnn_W_left, L1_gnn_W_right, L1_gnn_W_lin, L1_gnn_b_lin, L1_gnn_ln_a, L1_gnn_ln_b), axis=-1)
    return x

_drawn_inputs = setup_inputs


def setup_inputs(seed=0):
    import zlib

    import numpy as np

    out = dict(_drawn_inputs(seed))
    spreads = {'L1_gnn_b_lin': (0.0, 0.1), 'L1_gnn_ln_a': (1.0, 0.2), 'L1_gnn_ln_b': (0.0, 0.1)}
    factors = {'L0_gnn_Wq': 8.0, 'L0_gnn_Wk': 8.0, 'L0_gnn_bv': 3.389}
    for name, (base, spread) in spreads.items():
        noise = np.random.default_rng([zlib.crc32(name.encode()), seed]).standard_normal(out[name].shape)
        drawn = base * np.exp(spread * noise) if base else spread * noise
        out[name] = jnp.asarray(drawn.astype(out[name].dtype))
    for name, factor in factors.items():
        out[name] = (out[name] * factor).astype(out[name].dtype)
    return out
```

```python
from contextlib import ExitStack

import concourse.bass as bass
from concourse import mybir

P = 128
F32 = mybir.dt.float32
F32R = mybir.dt.float32r
ALU = mybir.AluOpType
ACT = mybir.ActivationFunctionType

LN_EPS = 1e-5
STD_EPS = 1e-3
SUM_EPS = 1e-10


def at(turn, per_turn, k):
    return turn * per_turn + k


def adj_resnorm_kernel(nc, x, adj, Wq, Wk, Wv, bv, Wo, bo, Wl, Wr, Wlin, b_lin, ln_a, ln_b, out):
    B, N, H = x.shape
    LAYERS = Wl.shape[0]
    HEADS = 12
    HD = H // HEADS
    NT = N // P
    HC = H // P
    PER = P // HD
    PAIRS = HEADS // 2
    SCALE = float(H) ** -0.5
    assert (NT, HC, PER, LAYERS) == (2, 3, 4, 2)

    MATS = [Wq, Wk, Wv, Wo] + [w[l] for l in range(LAYERS) for w in (Wl, Wr, Wlin)]
    Q_, K_, V_, O_ = range(4)
    LEFT, RIGHT, LIN = (lambda l: 4 + 3 * l), (lambda l: 5 + 3 * l), (lambda l: 6 + 3 * l)
    BIAS = [bv, bo] + [b_lin[l] for l in range(LAYERS)]
    BV, BO, BL = 0, 1, 2
    VAL = [0, 128, 224, 352]
    SLOT = [VAL[j] - HD * j for j in range(PER)]
    VW = VAL[-1] + HD
    NSTAGE = 5

    with ExitStack() as ctx:
        def sb(name, shape, dt=F32):
            return ctx.enter_context(nc.sbuf_tensor(name, shape, dt))

        def sem(name):
            return ctx.enter_context(nc.semaphore(name))

        w_hi = sb("w_hi", [P, len(MATS), HC, H], F32R)
        w_lo = sb("w_lo", [P, len(MATS), HC, H], F32R)
        ident = sb("ident", [P, P])
        power = sb("power", [P, 2, NT])
        a_col = sb("a_col", [P, HC])
        b_col = sb("b_col", [P, HC])
        a_row = sb("a_row", [P, H])
        b_row = sb("b_row", [P, H])
        xin = sb("xin", [P, NT, H])
        adj_in = sb("adj_in", [P, NT, N])
        xo_hi = sb("xo_hi", [P, HC, N], F32R)
        xo_lo = sb("xo_lo", [P, HC, N], F32R)
        qk_part = sb("qk_part", [P, 2, 4, N], F32R)
        pt_hi = qk_part[:, 0, :, :]
        pt_lo = qk_part[:, 1, :, :]
        stack = sb("stack", [P, 2, HEADS, N], F32R)
        SR = 3 * HD
        v_hi = sb("v_hi", [P, NT, HC, VW], F32R)
        v_lo = sb("v_lo", [P, NT, HC, VW], F32R)
        prob = sb("prob", [P, 2, 2, NT, N])
        junk = sb("junk", [P, NT, N], mybir.dt.bfloat16)
        nmax = sb("nmax", [P, HEADS, NT])
        asum = sb("asum", [P, HEADS, NT])
        esum = sb("esum", [P, HEADS, NT])
        rsum = sb("rsum", [P, HEADS, NT])
        x1 = sb("x1", [P, NT, H])
        stat_a = sb("stat_a", [P, NT, 8])
        rstd_a = sb("rstd_a", [P, NT])
        x1_res = sb("x1_res", [P, NT, H])
        adjT = sb("adjT", [P, NT, N])
        mask = sb("mask", [P, NT, 3 * P])
        h_hi = sb("h_hi", [P, HC, N], F32R)
        h_lo = sb("h_lo", [P, HC, N], F32R)
        m_hi = sb("m_hi", [P, 2 * HC, N], F32R)
        m_lo = sb("m_lo", [P, 2 * HC, N], F32R)
        l_hi = sb("l_hi", [P, NT, H + 2], F32R)
        l_lo = sb("l_lo", [P, NT, H + 2], F32R)
        um = sb("um", [P, NT, 3 * P])
        hT = um[:, :, :].rearrange("p a b -> p (a b)").rearrange("p (c n) -> p c n", c=HC)
        ex = sb("ex", [P, NT, N])
        e_hi = m_hi[:, 0:NT, :]
        e_lo = m_lo[:, 0:NT, :]
        cz = sb("cz", [P, NT, H])
        stat_b = sb("stat_b", [P, NT, 8])
        den = sb("den", [P, NT])
        rden = sb("rden", [P, NT])
        std_b = sb("std_b", [P, NT])
        rstd_b = sb("rstd_b", [P, NT])
        def bias_at(first, second, n):
            return (first, second)[n // 2][0:1].rearrange("p a b -> p (a b)")[:, n % 2 * H:(n % 2 + 1) * H]

        bias_raw = [bias_at(cz[:, :, :], um[:, :, :], n) for n in range(len(BIAS))]
        bias_hi = [bias_at(xo_hi[:, :, :], h_hi[:, :, :], n) for n in range(len(BIAS))]
        bias_lo = [bias_at(xo_lo[:, :, :], h_lo[:, :, :], n) for n in range(len(BIAS))]
        wstage = prob[:, :, :, :, :].rearrange("p a b c d -> p (a b c d)")

        bank = [ctx.enter_context(nc.psum_tensor(f"bank{i}", [P, 512], F32)) for i in range(8)]
        ov_bank = bank[4]
        s_w = [sem(f"weight_landed{i}") for i in range(NSTAGE)]
        s_wt = sem("weight_turned")
        s_whi = sem("weight_hi")
        s_wlo = sem("weight_lo")
        s_id = sem("identity_made")
        s_bias = sem("bias_landed")
        s_bhi = sem("bias_hi")
        s_blo = sem("bias_lo")
        s_brow = sem("bias_rows_placed")
        s_col = sem("ln_vectors_landed")
        s_zero = sem("padding_made")
        s_pow = sem("exponents_made")
        passed = {nc.vector.engine: sem("vector_wait_passed"), nc.gpsimd.engine: sem("gpsimd_wait_passed")}
        x_in = sem("x_landed")
        adj_ld = sem("adj_landed")
        x_res = sem("x_residual_landed")
        xt_full = sem("xt_in_psum")
        xt_hi = sem("xt_hi_done")
        xt_lo = sem("xt_lo_done")
        qk_full = sem("qk_in_psum")
        qk_hi = sem("qk_hi_done")
        qk_lo = sem("qk_lo_done")
        stacked = [sem(f"stacked{c}") for c in range(HC)]
        v_full = sem("v_in_psum")
        v_hi_s = sem("v_hi_done")
        v_lo_s = sem("v_lo_done")
        s_full = sem("scores_in_psum")
        s_neg = sem("scores_negated")
        s_abs = sem("scores_abs_summed")
        s_exp = sem("exp_done")
        s_rec = sem("esum_inverted")
        s_nz = sem("zero_rows_found")
        s_rn = sem("row_factor_ready")
        s_norm = sem("probs_normalised")
        pt_full = sem("pt_in_psum")
        pt_hi_s = sem("pt_hi_done")
        pt_lo_s = sem("pt_lo_done")
        pv_used = sem("pv_products_done")
        ot_full = sem("heads_out_in_psum")
        ot_hi = sem("heads_out_hi_done")
        ot_lo = sem("heads_out_lo_done")
        o_full = sem("o_in_psum")
        o_sum = sem("residual_added")
        a_stat = sem("x1_stats")
        a_aggr = sem("x1_stats_joined")
        a_var = sem("x1_var_ready")
        a_rstd = sem("x1_rstd")
        x1_ready = sem("x1_ready")
        at_full = sem("adjt_in_psum")
        at_done = sem("adjt_copied")
        masks = sem("masks_made")
        res_kept = sem("x1_residual_kept")
        t_full = sem("ht_in_psum")
        h_f32 = sem("ht_relu_done")
        h_hi_s = sem("h_hi_done")
        h_lo_s = sem("h_lo_done")
        m_full = sem("m_in_psum")
        m_hi_s = sem("m_hi_done")
        m_lo_s = sem("m_lo_done")
        l_full = sem("hlin_in_psum")
        l_hi_s = sem("hlin_hi_done")
        l_lo_s = sem("hlin_lo_done")
        u_full = sem("u_in_psum")
        u_mask = sem("u_masked")
        u_add = sem("u_halves_added")
        u_exp = sem("u_exp_done")
        u_adj = sem("u_exp_times_adj")
        e_hi_s = sem("e_hi_done")
        e_lo_s = sem("e_lo_done")
        c_full = sem("ctx_in_psum")
        c_den = sem("ctx_den_ready")
        c_rden = sem("ctx_rden_ready")
        c_copy = sem("ctx_scaled")
        b_stat = sem("ctx_stats")
        b_aggr = sem("ctx_stats_joined")
        b_var = sem("ctx_var_ready")
        b_std = sem("ctx_std")
        b_stde = sem("ctx_std_plus_eps")
        b_rstd = sem("ctx_rstd")
        z_ready = sem("ctx_normalised")
        f_mul = sem("final_scaled")
        f_add = sem("final_shifted")
        f_res = sem("final_residual_added")
        f_stat = sem("final_stats")
        f_aggr = sem("final_stats_joined")
        f_var = sem("final_var_ready")
        f_rstd = sem("final_rstd")
        f_out = sem("final_ready")
        stored = sem("out_stored")

        LAYER = ["T0", "T1", "M0", "M1", "M2", "L0", "L1", "U0", "U1", "C0", "C1"]
        UNITS = [(l, u) for l in range(LAYERS) for u in LAYER]
        LAST = {"T0": (h_lo_s, 4, 1), "T1": (h_lo_s, 4, 2), "M0": (m_lo_s, 6, 1), "M1": (m_lo_s, 6, 2),
                "M2": (m_lo_s, 6, 3), "L0": (l_lo_s, 4, 1), "L1": (l_lo_s, 4, 2), "U0": (u_mask, 4, 1),
                "U1": (u_mask, 4, 2), "C0": (c_copy, 4, 1), "C1": (c_copy, 4, 2)}

        def b_bank(l, u):
            return bank[5 + UNITS.index((l, u)) % 3]

        def b_bank_free(pe, l, u, tb, first):
            i = UNITS.index((l, u))
            before = [k for k in range(len(UNITS)) if k % 3 == i % 3]
            n = before.index(i)
            pl, pu = UNITS[before[n - 1]]
            s, per, k = LAST[pu]
            if n > 0:
                pe.wait_ge(s, at(tb, per, pl * per // LAYERS + k))
            elif not first:
                pe.wait_ge(s, at(tb - 1, per, pl * per // LAYERS + k))

        def r32(ap):
            return ap.bitcast(F32)

        def v_view(v, n, a):
            o = VAL[2 * a]
            return v[:, n, :, o:o + 160].rearrange("p c (j w) -> p c j w", w=32)[:, :, 0:5:4, :]

        def v_src(n, a):
            return bank[1 + n][:, 0:H].rearrange("p (c j w) -> p c j w", c=HC, w=HD)[:, :, 2 * a:2 * a + 2, :]

        ORDER = [
            "XT", ("QK", 0), ("t", 0), "keep", ("QK", 1), ("m", 0, 0), ("QK", 2), ("m", 0, 1), ("m", 0, 2),
            "V", ("l", 0), ("S", 0), ("u", 0), ("S", 1), ("N", 0), ("e", 0), ("T", 0),
            ("S", 2), ("N", 1), ("PV", 0), ("T", 1), ("c", 0), ("S", 3), ("N", 2), ("z", 0), ("PV", 1), ("T", 2),
            ("t", 1), ("S", 4), ("N", 3), ("m", 1, 0), ("PV", 2), ("m", 1, 1), ("T", 3), ("m", 1, 2), ("l", 1),
            ("S", 5), ("N", 4), ("PV", 3), ("T", 4), ("u", 1), ("N", 5), ("PV", 4), ("e", 1), ("T", 5),
            ("c", 1), ("PV", 5), "AT", ("z", 1), "O", "fin",
        ]

        def steps(do_a, do_b):
            for s in ORDER:
                name = s if isinstance(s, str) else s[0]
                if do_a if name.isupper() else do_b:
                    yield name, (() if isinstance(s, str) else s[1:])

        def turns(eng, body):
            body(0, None, True, False, True, False, True)
            body(1, 0, True, True, False, True, True)
            with eng.Fori(2, B - 1) as t:
                body(t, t - 1, True, True, False, False, True)
            body(B - 1, B - 2, True, True, False, False, False)
            body(None, B - 1, False, True, False, False, False)

        def wait_apart(eng, s, value):
            eng.wait_ge(s, value)
            eng.sem_inc(passed[eng.engine], 1)

        block = ctx.enter_context(nc.Block())

        @block.sync
        def _(sp):
            def load_x(t):
                sp.dma_start(xin[:, :, :], x[t, :, :].rearrange("(n p) h -> p n h", p=P)).then_inc(x_in, 16)

            def load_adj(t):
                sp.dma_start(adj_in[:, :, :], adj[t, :, :].rearrange("(n p) m -> p n m", p=P)).then_inc(adj_ld, 16)

            for i in range(len(MATS) * HC):
                if i >= NSTAGE:
                    sp.wait_ge(s_wt, i - NSTAGE + 1)
                sp.dma_start(wstage[:, i % NSTAGE * H:(i % NSTAGE + 1) * H],
                             MATS[i // HC][i % HC * P:(i % HC + 1) * P, :]).then_inc(s_w[i % NSTAGE], 16)
                if i == 2:
                    load_x(0)
                    load_adj(0)
                if i == NSTAGE - 1:
                    for n, b in enumerate(BIAS):
                        sp.dma_start(bias_raw[n], b.rearrange("(a h) -> a h", a=1)).then_inc(s_bias, 16)
                    sp.dma_start(a_col[:, :], ln_a[0, :].rearrange("(c p) -> p c", p=P),
                                 allow_slow_non_contiguous=True).then_inc(s_col, 16)
                    sp.dma_start(b_col[:, :], ln_b[0, :].rearrange("(c p) -> p c", p=P),
                                 allow_slow_non_contiguous=True).then_inc(s_col, 16)
                    sp.dma_start(a_row[:, :], ln_a[1, :].partition_broadcast(P)).then_inc(s_col, 16)
                    sp.dma_start(b_row[:, :], ln_b[1, :].partition_broadcast(P)).then_inc(s_col, 16)
            sp.wait_ge(s_blo, len(BIAS))
            for n in range(len(BIAS)):
                for part, row in ((bias_hi, SR), (bias_lo, SR + 1)):
                    sp.dma_start(r32(stack[row:row + 1, 0, 2 * n:2 * n + 2, :].rearrange("p a b -> p (a b)")[:, 0:H]),
                                 r32(part[n])).then_inc(s_brow, 16)

            def body(ta, tb, do_a, do_b, first_a, first_b, more):
                for name, arg in steps(do_a, do_b):
                    if name == "XT" and more:
                        sp.wait_ge(xt_full, at(ta, 2, 2))
                        load_x(ta + 1)
                    if name == "QK":
                        c, = arg
                        sp.wait_ge(qk_lo, at(ta, HC, c + 1))
                        part = qk_part[:, c % 2, :, :]
                        for j in range(PER):
                            src = part[HD * j:HD * (j + 1), :, :]
                            h = PER * c + j
                            for r, (a, step) in enumerate(((0, 2), (0, 3), (1, 1))):
                                sp.dma_start(r32(stack[HD * r:HD * (r + 1), :, h, :]),
                                             r32(src[:, a:a + step + 1:step, :])).then_inc(stacked[c], 16)
                    if name == "V":
                        if not first_a:
                            sp.wait_ge(res_kept, at(ta - 1, 1, 1))
                        sp.dma_start(x1[:, :, :], x[ta, :, :].rearrange("(n p) h -> p n h", p=P)).then_inc(x_res, 16)
                    if name == "AT" and more:
                        sp.wait_ge(masks, at(ta, 1, 1))
                        load_adj(ta + 1)
                    if name == "fin":
                        sp.wait_ge(f_out, at(tb, 2, 2))
                        sp.dma_start(out[tb, :, :].rearrange("(n p) h -> p n h", p=P), cz[:, :, :]).then_inc(stored, 16)

            turns(sp, body)
            sp.wait_ge(stored, 16 * B)

        @block.tensor
        def _(pe):
            def mm3(o, lh, ll, rh, rl, start, stop):
                pe.matmul(o, lh, rh, start=start, stop=False)
                pe.matmul(o, lh, rl, start=False, stop=False)
                return pe.matmul(o, ll, rh, start=False, stop=stop)

            def bias(o, n, start):
                return pe.matmul(o, stack[SR:SR + 2, 1, 0, 0:P],
                                 stack[SR:SR + 2, 0, 2 * n:2 * n + 2, :].rearrange("p a b -> p (a b)")[:, 0:H],
                                 start=start, stop=False)

            pe.wait_ge(s_id, 2)
            for i in range(len(MATS) * HC):
                pe.wait_ge(s_w[i % NSTAGE], 16 * (i // NSTAGE + 1))
                if i >= 4:
                    pe.wait_ge(s_wlo, i - 3)
                for c in range(HC):
                    o = i % NSTAGE * H + c * P
                    mm = pe.transpose(bank[i % 4][:, c * P:(c + 1) * P], wstage[:, o:o + P], ident[:, :])
                mm.then_inc(s_wt, 1)
            pe.wait_ge(s_wlo, len(MATS) * HC)
            pe.wait_ge(s_brow, 16 * 2 * len(BIAS))
            pe.wait_ge(s_zero, 5)

            def body(ta, tb, do_a, do_b, first_a, first_b, more):
                for name, arg in steps(do_a, do_b):
                    if name == "XT":
                        pe.wait_ge(x_in, at(ta, 16, 16))
                        for u, cs in enumerate(((0, 1), (2,))):
                            if not first_a:
                                pe.wait_ge(o_sum, at(ta - 1, 2, u + 1))
                            for c in cs:
                                for n in range(NT):
                                    mm = pe.transpose(bank[u][:, (c % 2) * N + n * P:(c % 2) * N + (n + 1) * P],
                                                      xin[:, n, c * P:(c + 1) * P], ident[:, :])
                            mm.then_inc(xt_full, 1)
                    if name == "QK":
                        m, = arg
                        if m == 0:
                            if not first_a:
                                pe.wait_ge(at_done, at(ta - 1, 1, 1))
                            pe.wait_ge(xt_lo, at(ta, 2, 2))
                        if m == 1 and not first_a:
                            pe.wait_ge(pt_lo_s, at(ta - 1, HEADS, HEADS))
                        b = bank[(2, 3, 0)[m]]
                        for half, w in enumerate((Q_, K_)):
                            for c in range(HC):
                                mm = mm3(b[:, half * N:(half + 1) * N],
                                         w_hi[:, w, c, m * P:(m + 1) * P], w_lo[:, w, c, m * P:(m + 1) * P],
                                         xo_hi[:, c, :], xo_lo[:, c, :], c == 0, c == HC - 1)
                        mm.then_inc(qk_full, 1)
                    if name == "V":
                        for n in range(NT):
                            if n == 1:
                                pe.wait_ge(qk_lo, at(ta, HC, 1))
                            o = bank[1 + n][:, 0:H]
                            bias(o, BV, True)
                            for c in range(HC):
                                mm = mm3(o, xo_hi[:, c, n * P:(n + 1) * P], xo_lo[:, c, n * P:(n + 1) * P],
                                         w_hi[:, V_, c, :], w_lo[:, V_, c, :], False, c == HC - 1)
                            mm.then_inc(v_full, 1)
                    if name == "S":
                        for h in (2 * arg[0], 2 * arg[0] + 1):
                            if h % PER == 0:
                                pe.wait_ge(stacked[h // PER], at(ta, 16 * 3 * PER, 16 * 3 * PER))
                            if h == 0:
                                pe.wait_ge(qk_lo, at(ta, HC, HC))
                            elif h == 1:
                                pe.wait_ge(v_lo_s, at(ta, 2 * NT, 2))
                            else:
                                pe.wait_ge(s_neg, at(ta, 2 * HEADS, 2 * (h - 1)))
                            for n in range(NT):
                                mm = pe.matmul(bank[h % 2][:, n * N:(n + 1) * N],
                                               stack[0:SR, 0, h, n * P:(n + 1) * P], stack[0:SR, 1, h, :],
                                               start=True, stop=True)
                            mm.then_inc(s_full, 1)
                    if name == "T":
                        g, = arg
                        pe.wait_ge(s_norm, at(ta, PAIRS, g + 1))
                        for i in range(2):
                            h = 2 * g + i
                            if h == 0:
                                pe.wait_ge(v_lo_s, at(ta, 2 * NT, 4))
                            elif h >= 2:
                                pe.wait_ge(pt_lo_s, at(ta, HEADS, h - 1))
                            for kt in range(NT):
                                for n in range(NT):
                                    mm = pe.transpose(bank[2 + i][:, kt * N + n * P:kt * N + (n + 1) * P],
                                                      prob[:, g % 2, i, n, kt * P:(kt + 1) * P], ident[:, :])
                            mm.then_inc(pt_full, 1)
                    if name == "PV":
                        g, = arg
                        c = g // 2
                        if g % 2 == 0:
                            if c > 0:
                                pe.wait_ge(ot_lo, at(ta, HC, c))
                            elif not first_a:
                                pe.wait_ge(ot_lo, at(ta - 1, HC, HC))
                        for i in range(2):
                            j = 2 * (g % 2) + i
                            pe.wait_ge(pt_lo_s, at(ta, HEADS, 2 * g + i + 1))
                            for kt in range(NT):
                                sl = slice(SLOT[j], SLOT[j] + P)
                                mm = mm3(ov_bank[:, 0:N], v_hi[:, kt, c, sl], v_lo[:, kt, c, sl],
                                         pt_hi[:, 2 * i + kt, :], pt_lo[:, 2 * i + kt, :],
                                         j == 0 and kt == 0, j == PER - 1 and kt == NT - 1)
                        mm.then_inc(pv_used, 1)
                    if name == "AT":
                        pe.wait_ge(pt_lo_s, at(ta, HEADS, HEADS - 1))
                        for J in range(NT):
                            for n in range(NT):
                                mm = pe.transpose(bank[2][:, J * N + n * P:J * N + (n + 1) * P],
                                                  adj_in[:, n, J * P:(J + 1) * P], ident[:, :])
                        mm.then_inc(at_full, 1)
                    if name == "O":
                        pe.wait_ge(s_neg, at(ta, 2 * HEADS, 2 * HEADS))
                        pe.wait_ge(ot_lo, at(ta, HC, HC))
                        for n in range(NT):
                            o = bank[n][:, 0:H]
                            bias(o, BO, True)
                            for c in range(HC):
                                mm = mm3(o, xo_hi[:, c, n * P:(n + 1) * P], xo_lo[:, c, n * P:(n + 1) * P],
                                         w_hi[:, O_, c, :], w_lo[:, O_, c, :], False, c == HC - 1)
                            mm.then_inc(o_full, 1)
                    if name == "t":
                        l, = arg
                        src = x1 if l == 0 else cz
                        if l == 0:
                            pe.wait_ge(x1_ready, at(tb, NT, NT))
                        else:
                            pe.wait_ge(z_ready, at(tb, 4, 2))
                        for u, cs in enumerate(((0, 1), (2,))):
                            b_bank_free(pe, l, f"T{u}", tb, first_b)
                            b = b_bank(l, f"T{u}")
                            for c in cs:
                                for n in range(NT):
                                    mm = pe.transpose(b[:, (c % 2) * N + n * P:(c % 2) * N + (n + 1) * P],
                                                      src[:, n, c * P:(c + 1) * P], ident[:, :])
                            mm.then_inc(t_full, 1)
                    if name == "m":
                        l, u = arg
                        b_bank_free(pe, l, f"M{u}", tb, first_b)
                        if u == 0:
                            pe.wait_ge(h_lo_s, at(tb, 4, 2 * l + 2))
                        b = b_bank(l, f"M{u}")
                        for half in range(2):
                            k = 2 * u + half
                            w, m = (LEFT(l), k) if k < HC else (RIGHT(l), k - HC)
                            for c in range(HC):
                                mm = mm3(b[:, half * N:(half + 1) * N],
                                         w_hi[:, w, c, m * P:(m + 1) * P], w_lo[:, w, c, m * P:(m + 1) * P],
                                         h_hi[:, c, :], h_lo[:, c, :], c == 0, c == HC - 1)
                        mm.then_inc(m_full, 1)
                    if name == "l":
                        l, = arg
                        for n in range(NT):
                            b_bank_free(pe, l, f"L{n}", tb, first_b)
                            o = b_bank(l, f"L{n}")[:, 0:H]
                            bias(o, BL + l, True)
                            for c in range(HC):
                                mm = mm3(o, h_hi[:, c, n * P:(n + 1) * P], h_lo[:, c, n * P:(n + 1) * P],
                                         w_hi[:, LIN(l), c, :], w_lo[:, LIN(l), c, :], False, c == HC - 1)
                            mm.then_inc(l_full, 1)
                    if name == "u":
                        l, = arg
                        pe.wait_ge(m_lo_s, at(tb, 6, 3 * l + 3))
                        for J in range(NT):
                            b_bank_free(pe, l, f"U{J}", tb, first_b)
                            b = b_bank(l, f"U{J}")
                            js = slice(J * P, (J + 1) * P)
                            for side, lo, hi, to in ((0, 0, (J + 1) * P, 0), (1, J * P, N, (J + 1) * P)):
                                for c in range(HC):
                                    mm = mm3(b[:, to:to + hi - lo], m_hi[:, side * HC + c, js],
                                             m_lo[:, side * HC + c, js], h_hi[:, c, lo:hi], h_lo[:, c, lo:hi],
                                             c == 0, c == HC - 1)
                            mm.then_inc(u_full, 1)
                    if name == "c":
                        l, = arg
                        pe.wait_ge(e_lo_s, at(tb, 2, l + 1))
                        pe.wait_ge(l_lo_s, at(tb, 4, 2 * l + 2))
                        for n in range(NT):
                            b_bank_free(pe, l, f"C{n}", tb, first_b)
                            b = b_bank(l, f"C{n}")
                            for J in range(NT):
                                mm = mm3(b[:, 0:H + 2], e_hi[:, J, n * P:(n + 1) * P], e_lo[:, J, n * P:(n + 1) * P],
                                         l_hi[:, J, :], l_lo[:, J, :], J == 0, J == NT - 1)
                            mm.then_inc(c_full, 1)

            turns(pe, body)

        @block.scalar
        def _(act):
            for i in range(len(MATS) * HC):
                act.wait_ge(s_wt, i + 1)
                act.activation(w_hi[:, i // HC, :, i % HC * P:(i % HC + 1) * P],
                               bank[i % 4][:, 0:H].rearrange("p (c o) -> p c o", c=HC), ACT.Copy,
                               scale=0.5 * SCALE if i // HC == Q_ else 1.0).then_inc(s_whi, 1)

            def body(ta, tb, do_a, do_b, first_a, first_b, more):
                for name, arg in steps(do_a, do_b):
                    if name == "XT":
                        if not first_a:
                            act.wait_ge(o_full, at(ta - 1, NT, NT))
                        for u, w in enumerate((2, 1)):
                            act.wait_ge(xt_full, at(ta, 2, u + 1))
                            act.activation(xo_hi[:, 2 * u:2 * u + w, :],
                                           bank[u][:, 0:w * N].rearrange("p (c n) -> p c n", c=w),
                                           ACT.Copy).then_inc(xt_hi, 1)
                    if name == "QK":
                        m, = arg
                        act.wait_ge(qk_full, at(ta, HC, m + 1))
                        if m == 0 and not first_a:
                            act.wait_ge(pv_used, at(ta - 1, PAIRS, PAIRS))
                        if m == 2:
                            act.wait_ge(stacked[0], at(ta, 16 * 3 * PER, 16 * 3 * PER))
                        act.activation(qk_part[:, m % 2, 0:3:2, :],
                                       bank[(2, 3, 0)[m]][:, :].rearrange("p (a n) -> p a n", a=2),
                                       ACT.Copy).then_inc(qk_hi, 1)
                    if name == "V":
                        if not first_a:
                            act.wait_ge(pv_used, at(ta - 1, PAIRS, PAIRS))
                        for n in range(NT):
                            act.wait_ge(v_full, at(ta, NT, n + 1))
                            for a in range(2):
                                act.activation(v_view(v_hi, n, a), v_src(n, a), ACT.Copy).then_inc(v_hi_s, 1)
                    if name == "S":
                        g, = arg
                        for h in (2 * g, 2 * g + 1):
                            for n in range(NT):
                                k = 2 * h + n
                                act.wait_ge(s_neg, at(ta, 2 * HEADS, k + 1))
                                if k >= 2:
                                    act.wait_ge(s_abs, at(ta, 2 * HEADS, k - 1))
                                elif not first_a:
                                    act.wait_ge(s_abs, at(ta - 1, 2 * HEADS, 2 * HEADS + k - 1))
                                act.activation(junk[:, n, :], prob[:, g % 2, h % 2, n, :], ACT.Abs,
                                               accum_out=asum[:, h, n:n + 1]).then_inc(s_abs, 1)
                            for n in range(NT):
                                p = prob[:, g % 2, h % 2, n, :]
                                act.wait_ge(s_abs, at(ta, 2 * HEADS, 2 * h + n + 1))
                                act.activation(p, p, ACT.Exp, bias=nmax[:, h, n:n + 1], scale=-1.0,
                                               accum_out=esum[:, h, n:n + 1]).then_inc(s_exp, 1)
                    if name == "T":
                        g, = arg
                        if g > 0:
                            act.wait_ge(pv_used, at(ta, PAIRS, g))
                        else:
                            act.wait_ge(stacked[1], at(ta, 16 * 3 * PER, 16 * 3 * PER))
                            act.wait_ge(stacked[2], at(ta, 16 * 3 * PER, 16 * 3 * PER))
                        for i in range(2):
                            act.wait_ge(pt_full, at(ta, HEADS, 2 * g + i + 1))
                            act.activation(pt_hi[:, 2 * i:2 * i + 2, :],
                                           bank[2 + i][:, :].rearrange("p (k n) -> p k n", k=NT),
                                           ACT.Copy).then_inc(pt_hi_s, 1)
                    if name == "PV" and arg[0] % 2 == 1:
                        c = arg[0] // 2
                        act.wait_ge(pv_used, at(ta, PAIRS, arg[0] + 1))
                        if c == 0:
                            act.wait_ge(v_full, at(ta, NT, NT))
                        act.activation(xo_hi[:, c, :], ov_bank[:, 0:N], ACT.Copy).then_inc(ot_hi, 1)
                    if name == "AT":
                        act.wait_ge(at_full, at(ta, 1, 1))
                        if not first_a:
                            act.wait_ge(u_adj, at(ta - 1, LAYERS, LAYERS))
                        act.activation(adjT[:, :, :], bank[2][:, :].rearrange("p (k n) -> p k n", k=NT),
                                       ACT.Copy).then_inc(at_done, 1)
                    if name == "t":
                        l, = arg
                        for u, w in enumerate((2, 1)):
                            act.wait_ge(t_full, at(tb, 4, 2 * l + u + 1))
                            b = b_bank(l, f"T{u}")
                            if l == 0:
                                if u == 0 and not first_b:
                                    act.wait_ge(u_full, at(tb - 1, 4, 4))
                                    act.wait_ge(l_full, at(tb - 1, 4, 4))
                                act.activation(h_hi[:, 2 * u:2 * u + w, :],
                                               b[:, 0:w * N].rearrange("p (c n) -> p c n", c=w),
                                               ACT.Copy).then_inc(h_hi_s, 1)
                            else:
                                for c in range(2 * u, 2 * u + w):
                                    if c == 0:
                                        act.wait_ge(s_col, 64)
                                        act.wait_ge(u_exp, at(tb, 4, 2))
                                    act.activation(hT[:, c, :], b[:, (c % 2) * N:(c % 2 + 1) * N], ACT.Relu,
                                                   scale=a_col[:, c:c + 1],
                                                   bias=b_col[:, c:c + 1]).then_inc(h_f32, 1)
                    if name == "m":
                        l, u = arg
                        act.wait_ge(m_full, at(tb, 6, 3 * l + u + 1))
                        if u == 0 and (l > 0 or not first_b):
                            act.wait_ge(c_full, at(tb, 4, 2) if l > 0 else at(tb - 1, 4, 4))
                        act.activation(m_hi[:, 2 * u:2 * u + 2, :],
                                       b_bank(l, f"M{u}")[:, :].rearrange("p (c n) -> p c n", c=2),
                                       ACT.Copy).then_inc(m_hi_s, 1)
                    if name == "l":
                        l, = arg
                        if l > 0 or not first_b:
                            act.wait_ge(c_full, at(tb, 4, 2) if l > 0 else at(tb - 1, 4, 4))
                        for n in range(NT):
                            act.wait_ge(l_full, at(tb, 4, 2 * l + n + 1))
                            act.activation(l_hi[:, n, 0:H], b_bank(l, f"L{n}")[:, 0:H],
                                           ACT.Copy).then_inc(l_hi_s, 1)
                    if name == "u":
                        l, = arg
                        for J in range(NT):
                            act.wait_ge(u_add, at(tb, 4, 2 * l + J + 1))
                            if J == 0 and (l > 0 or not first_b):
                                act.wait_ge(e_lo_s, at(tb, 2, 1) if l > 0 else at(tb - 1, 2, 2))
                            act.activation(ex[:, J, :], um[:, J, (1 - J) * P:(1 - J) * P + N], ACT.Exp,
                                           scale=SCALE).then_inc(u_exp, 1)
                    if name == "e":
                        l, = arg
                        act.wait_ge(u_adj, at(tb, LAYERS, l + 1))
                        act.wait_ge(u_full, at(tb, 4, 2 * l + 2))
                        act.activation(e_hi, ex[:, :, :], ACT.Copy).then_inc(e_hi_s, 1)
                    if name == "c":
                        l, = arg
                        if l == 0 and not first_b:
                            act.wait_ge(stored, at(tb - 1, 16, 16))
                        if l == 1:
                            act.wait_ge(t_full, at(tb, 4, 4))
                        for n in range(NT):
                            act.wait_ge(c_rden, at(tb, 4, 2 * l + n + 1))
                            act.activation(cz[:, n, :], b_bank(l, f"C{n}")[:, 0:H], ACT.Copy,
                                           scale=rden[:, n:n + 1]).then_inc(c_copy, 1)

            turns(act, body)

        @block.vector
        def _(dve):
            dve.memset(r32(stack[SR:P, 1, 0, 0:P]), 1.0).then_inc(s_zero, 1)
            dve.wait_ge(s_bias, 16 * len(BIAS))
            for n in range(len(BIAS)):
                dve.tensor_copy(bias_hi[n], bias_raw[n]).then_inc(s_bhi, 1)
            dve.wait_ge(s_bhi, len(BIAS))
            for n in range(len(BIAS)):
                dve.tensor_tensor(bias_lo[n], bias_raw[n], r32(bias_hi[n]), ALU.subtract).then_inc(s_blo, 1)
            for i in range(len(MATS) * HC):
                dst = slice(i % HC * P, (i % HC + 1) * P)
                dve.wait_ge(s_whi, i + 1)
                dve.scalar_tensor_tensor(out=w_lo[:, i // HC, :, dst],
                                         in0=bank[i % 4][:, 0:H].rearrange("p (c o) -> p c o", c=HC),
                                         scalar=0.5 * SCALE if i // HC == Q_ else 1.0,
                                         in1=r32(w_hi[:, i // HC, :, dst]),
                                         op0=ALU.mult, op1=ALU.subtract).then_inc(s_wlo, 1)

            def body(ta, tb, do_a, do_b, first_a, first_b, more):
                for name, arg in steps(do_a, do_b):
                    if name == "XT":
                        for u, w in enumerate((2, 1)):
                            dve.wait_ge(xt_hi, at(ta, 2, u + 1))
                            dve.tensor_tensor(xo_lo[:, 2 * u:2 * u + w, :],
                                              bank[u][:, 0:w * N].rearrange("p (c n) -> p c n", c=w),
                                              r32(xo_hi[:, 2 * u:2 * u + w, :]), ALU.subtract).then_inc(xt_lo, 1)
                    if name == "QK":
                        m, = arg
                        dve.wait_ge(qk_hi, at(ta, HC, m + 1))
                        dve.tensor_tensor(qk_part[:, m % 2, 1:4:2, :],
                                          bank[(2, 3, 0)[m]][:, :].rearrange("p (a n) -> p a n", a=2),
                                          r32(qk_part[:, m % 2, 0:3:2, :]), ALU.subtract).then_inc(qk_lo, 1)
                    if name == "V":
                        for n in range(NT):
                            dve.wait_ge(v_hi_s, at(ta, 2 * NT, 2 * n + 2))
                            for a in range(2):
                                dve.tensor_tensor(v_view(v_lo, n, a), v_src(n, a), r32(v_view(v_hi, n, a)),
                                                  ALU.subtract).then_inc(v_lo_s, 1)
                    if name == "S":
                        g, = arg
                        if g == 0:
                            dve.wait_ge(adj_ld, at(ta, 16, 16))
                            if not first_a:
                                dve.wait_ge(pt_full, at(ta - 1, HEADS, HEADS))
                        elif g >= 2:
                            dve.wait_ge(pt_full, at(ta, HEADS, 2 * g - 2))
                        for i in range(2):
                            h = 2 * g + i
                            wait_apart(dve, s_full, at(ta, HEADS, h + 1))
                            for n in range(NT):
                                dve.tensor_tensor_reduce(prob[:, g % 2, i, n, :], bank[h % 2][:, n * N:(n + 1) * N],
                                                         adj_in[:, n, :], -2.0, 3.0e38, ALU.add, ALU.min,
                                                         nmax[:, h, n:n + 1]).then_inc(s_neg, 1)
                    if name == "N":
                        g, = arg
                        hs = slice(2 * g, 2 * g + 2)
                        dve.wait_ge(s_exp, at(ta, 2 * HEADS, 4 * g + 4))
                        dve.reciprocal(rsum[:, hs, :], esum[:, hs, :]).then_inc(s_rec, 1)
                        dve.wait_ge(s_rec, at(ta, PAIRS, g + 1))
                        dve.scalar_tensor_tensor(out=rsum[:, hs, :], in0=asum[:, hs, :], scalar=0.0,
                                                 in1=rsum[:, hs, :], op0=ALU.not_equal,
                                                 op1=ALU.mult).then_inc(s_rn, 1)
                    if name == "T":
                        g, = arg
                        for i in range(2):
                            dve.wait_ge(pt_hi_s, at(ta, HEADS, 2 * g + i + 1))
                            dve.tensor_tensor(pt_lo[:, 2 * i:2 * i + 2, :],
                                              bank[2 + i][:, :].rearrange("p (k n) -> p k n", k=NT),
                                              r32(pt_hi[:, 2 * i:2 * i + 2, :]), ALU.subtract).then_inc(pt_lo_s, 1)
                    if name == "PV" and arg[0] % 2 == 1:
                        c = arg[0] // 2
                        dve.wait_ge(ot_hi, at(ta, HC, c + 1))
                        dve.tensor_tensor(xo_lo[:, c, :], ov_bank[:, 0:N], r32(xo_hi[:, c, :]),
                                          ALU.subtract).then_inc(ot_lo, 1)
                    if name == "O":
                        dve.wait_ge(x_res, at(ta, 16, 16))
                        for n in range(NT):
                            dve.wait_ge(o_full, at(ta, NT, n + 1))
                            dve.tensor_tensor(x1[:, n, :], bank[n][:, 0:H], x1[:, n, :], ALU.add).then_inc(o_sum, 1)
                        for n in range(NT):
                            dve.wait_ge(o_sum, at(ta, NT, n + 1))
                            dve.bn_stats(stat_a[:, n, 0:6], x1[:, n, :]).then_inc(a_stat, 1)
                        wait_apart(dve, a_stat, at(ta, NT, NT))
                        for n in range(NT):
                            dve.bn_aggr(stat_a[:, n, 6:8], stat_a[:, n, 0:6]).then_inc(a_aggr, 1)
                        dve.wait_ge(a_aggr, at(ta, NT, NT))
                        dve.tensor_scalar(rstd_a[:, :], stat_a[:, :, 7], LN_EPS, None,
                                          ALU.add).then_inc(a_var, 1)
                        dve.wait_ge(a_rstd, at(ta, 1, 1))
                        for n in range(NT):
                            dve.tensor_scalar(x1[:, n, :], x1[:, n, :], stat_a[:, n, 6:7], rstd_a[:, n:n + 1],
                                              ALU.subtract, ALU.mult).then_inc(x1_ready, 1)
                    if name == "t":
                        l, = arg
                        for u, w in enumerate((2, 1)):
                            hs = slice(2 * u, 2 * u + w)
                            if l == 0:
                                dve.wait_ge(h_hi_s, at(tb, 4, u + 1))
                                dve.tensor_tensor(h_lo[:, hs, :],
                                                  b_bank(l, f"T{u}")[:, 0:w * N].rearrange("p (c n) -> p c n", c=w),
                                                  r32(h_hi[:, hs, :]), ALU.subtract).then_inc(h_lo_s, 1)
                            else:
                                dve.wait_ge(h_f32, at(tb, HC, 2 * u + w))
                                if u == 0:
                                    dve.wait_ge(u_full, at(tb, 4, 2))
                                    dve.wait_ge(l_full, at(tb, 4, 2))
                                dve.tensor_copy(h_hi[:, hs, :], hT[:, hs, :]).then_inc(h_hi_s, 1)
                                dve.wait_ge(h_hi_s, at(tb, 4, 2 + u + 1))
                                dve.tensor_tensor(h_lo[:, hs, :], hT[:, hs, :], r32(h_hi[:, hs, :]),
                                                  ALU.subtract).then_inc(h_lo_s, 1)
                    if name == "m":
                        l, u = arg
                        dve.wait_ge(m_hi_s, at(tb, 6, 3 * l + u + 1))
                        dve.tensor_tensor(m_lo[:, 2 * u:2 * u + 2, :],
                                          b_bank(l, f"M{u}")[:, :].rearrange("p (c n) -> p c n", c=2),
                                          r32(m_hi[:, 2 * u:2 * u + 2, :]), ALU.subtract).then_inc(m_lo_s, 1)
                    if name == "l":
                        l, = arg
                        for n in range(NT):
                            dve.wait_ge(l_hi_s, at(tb, 4, 2 * l + n + 1))
                            dve.tensor_tensor(l_lo[:, n, 0:H], b_bank(l, f"L{n}")[:, 0:H], r32(l_hi[:, n, 0:H]),
                                              ALU.subtract).then_inc(l_lo_s, 1)
                    if name == "u":
                        l, = arg
                        if l == 0:
                            dve.wait_ge(masks, at(tb, 1, 1))
                            if not first_b:
                                dve.wait_ge(u_exp, at(tb - 1, 4, 4))
                        else:
                            dve.wait_ge(h_lo_s, at(tb, 4, 4))
                        for J in range(NT):
                            dve.wait_ge(u_full, at(tb, 4, 2 * l + J + 1))
                            dve.tensor_tensor(um[:, J, :], b_bank(l, f"U{J}")[:, 0:3 * P], mask[:, J, :],
                                              ALU.mult).then_inc(u_mask, 1)
                        for J in range(NT):
                            dve.wait_ge(u_mask, at(tb, 4, 2 * l + J + 1))
                            o = 2 * J * P
                            dve.tensor_tensor(um[:, J, P:2 * P], um[:, J, P:2 * P], um[:, J, o:o + P],
                                              ALU.add).then_inc(u_add, 1)
                    if name == "e":
                        l, = arg
                        dve.wait_ge(e_hi_s, at(tb, 2, l + 1))
                        dve.tensor_tensor(e_lo, ex[:, :, :], r32(e_hi), ALU.subtract).then_inc(e_lo_s, 1)
                    if name == "c":
                        l, = arg
                        for n in range(NT):
                            dve.wait_ge(c_full, at(tb, 4, 2 * l + n + 1))
                            if n == 0 and (l > 0 or not first_b):
                                dve.wait_ge(c_copy, at(tb, 4, 2) if l > 0 else at(tb - 1, 4, 4))
                            dve.tensor_scalar(den[:, n:n + 1], b_bank(l, f"C{n}")[:, H:H + 1], SUM_EPS, None,
                                              ALU.add).then_inc(c_den, 1)
                            dve.wait_ge(c_den, at(tb, 4, 2 * l + n + 1))
                            dve.reciprocal(rden[:, n:n + 1], den[:, n:n + 1]).then_inc(c_rden, 1)
                    if name == "z":
                        l, = arg
                        for n in range(NT):
                            dve.wait_ge(c_copy, at(tb, 4, 2 * l + n + 1))
                            dve.bn_stats(stat_b[:, n, 0:6], cz[:, n, :]).then_inc(b_stat, 1)
                        wait_apart(dve, b_stat, at(tb, 4, 2 * l + 2))
                        for n in range(NT):
                            dve.bn_aggr(stat_b[:, n, 6:8], stat_b[:, n, 0:6]).then_inc(b_aggr, 1)
                        dve.wait_ge(b_aggr, at(tb, 4, 2 * l + 2))
                        dve.tensor_scalar(std_b[:, :], stat_b[:, :, 7], H / (H - 1.0), None,
                                          ALU.mult).then_inc(b_var, 1)
                        dve.wait_ge(b_std, at(tb, 2, l + 1))
                        dve.tensor_scalar(std_b[:, :], std_b[:, :], STD_EPS, None, ALU.add).then_inc(b_stde, 1)
                        dve.wait_ge(b_stde, at(tb, 2, l + 1))
                        dve.reciprocal(rstd_b[:, :], std_b[:, :]).then_inc(b_rstd, 1)
                        dve.wait_ge(b_rstd, at(tb, 2, l + 1))
                        for n in range(NT):
                            dve.tensor_scalar(cz[:, n, :], cz[:, n, :], stat_b[:, n, 6:7], rstd_b[:, n:n + 1],
                                              ALU.subtract, ALU.mult).then_inc(z_ready, 1)
                    if name == "fin":
                        dve.wait_ge(res_kept, at(tb, 1, 1))
                        for n in range(NT):
                            dve.wait_ge(f_add, at(tb, NT, n + 1))
                            dve.scalar_tensor_tensor(out=cz[:, n, :], in0=cz[:, n, :], scalar=0.0,
                                                     in1=x1_res[:, n, :], op0=ALU.max,
                                                     op1=ALU.add).then_inc(f_res, 1)
                        for n in range(NT):
                            dve.wait_ge(f_res, at(tb, NT, n + 1))
                            dve.bn_stats(stat_b[:, n, 0:6], cz[:, n, :]).then_inc(f_stat, 1)
                        wait_apart(dve, f_stat, at(tb, NT, NT))
                        for n in range(NT):
                            dve.bn_aggr(stat_b[:, n, 6:8], stat_b[:, n, 0:6]).then_inc(f_aggr, 1)
                        dve.wait_ge(f_aggr, at(tb, NT, NT))
                        dve.tensor_scalar(std_b[:, :], stat_b[:, :, 7], LN_EPS, None,
                                          ALU.add).then_inc(f_var, 1)
                        dve.wait_ge(f_rstd, at(tb, 1, 1))
                        for n in range(NT):
                            dve.tensor_scalar(cz[:, n, :], cz[:, n, :], stat_b[:, n, 6:7], std_b[:, n:n + 1],
                                              ALU.subtract, ALU.mult).then_inc(f_out, 1)

            turns(dve, body)

        @block.gpsimd
        def _(pool):
            pool.memset(ident[:, :], 0.0).then_inc(s_id, 1)
            pool.wait_ge(s_id, 1)
            pool.affine_select(out=ident[:, :], in_=ident[:, :], compare_op=ALU.not_equal, fill=1.0, base=0,
                               pattern=[[-1, P]], channel_multiplier=1).then_inc(s_id, 1)
            pool.memset(power[:, 0, :], -0.5).then_inc(s_pow, 1)
            pool.memset(power[:, 1, :], 0.5).then_inc(s_pow, 1)
            pool.wait_ge(s_pow, 2)
            pool.memset(r32(v_hi[:, :, :, :]), 0.0).then_inc(s_zero, 1)
            pool.memset(r32(v_lo[:, :, :, :]), 0.0).then_inc(s_zero, 1)
            pool.memset(r32(l_hi[:, :, H:H + 2]), 1.0).then_inc(s_zero, 1)
            pool.memset(r32(l_lo[:, :, H:H + 2]), 0.0).then_inc(s_zero, 1)
            pool.wait_ge(s_col, 64)

            def body(ta, tb, do_a, do_b, first_a, first_b, more):
                for name, arg in steps(do_a, do_b):
                    if name == "N":
                        g, = arg
                        wait_apart(pool, s_rn, at(ta, PAIRS, g + 1))
                        for i in range(2):
                            for n in range(NT):
                                p = prob[:, g % 2, i, n, :]
                                ins = pool.tensor_scalar(p, p, rsum[:, 2 * g + i, n:n + 1], None, ALU.mult)
                        ins.then_inc(s_norm, 1)
                    if name == "AT":
                        pool.wait_ge(at_done, at(ta, 1, 1))
                        if not first_a:
                            wait_apart(pool, u_mask, at(ta - 1, 4, 4))
                        for o, src, cm, st, base, w in (
                                (mask[:, 0, 0:P], adjT[:, 0, 0:P], 1, -1, 0, P),
                                (mask[:, 0, P:3 * P], adj_in[:, 0, :], -1, 1, -1, N),
                                (mask[:, 1, 0:2 * P], adjT[:, 1, :], 1, -1, P, N),
                                (mask[:, 1, 2 * P:3 * P], adj_in[:, 1, P:N], -1, 1, -1, P)):
                            ins = pool.affine_select(out=o, in_=src, compare_op=ALU.is_ge, fill=0.0, base=base,
                                                     pattern=[[st, w]], channel_multiplier=cm)
                        ins.then_inc(masks, 1)
                    if name == "O":
                        pool.wait_ge(a_var, at(ta, 1, 1))
                        pool.tensor_tensor(rstd_a[:, :], rstd_a[:, :], power[:, 0, :], ALU.pow).then_inc(a_rstd, 1)
                    if name == "z":
                        l, = arg
                        pool.wait_ge(b_var, at(tb, 2, l + 1))
                        pool.tensor_tensor(std_b[:, :], std_b[:, :], power[:, 1, :], ALU.pow).then_inc(b_std, 1)
                    if name == "keep":
                        pool.wait_ge(t_full, at(tb, 4, 2))
                        if not first_b:
                            wait_apart(pool, f_res, at(tb - 1, NT, NT))
                        pool.tensor_copy(x1_res[:, :, :], x1[:, :, :]).then_inc(res_kept, 1)
                    if name == "e":
                        l, = arg
                        pool.wait_ge(u_exp, at(tb, 4, 2 * l + 2))
                        pool.tensor_tensor(ex[:, :, :], ex[:, :, :], adjT[:, :, :], ALU.mult).then_inc(u_adj, 1)
                    if name == "fin":
                        for n in range(NT):
                            pool.wait_ge(z_ready, at(tb, 4, 2 + n + 1))
                            pool.tensor_tensor(cz[:, n, :], cz[:, n, :], a_row[:, :], ALU.mult).then_inc(f_mul, 1)
                            pool.wait_ge(f_mul, at(tb, NT, n + 1))
                            pool.tensor_tensor(cz[:, n, :], cz[:, n, :], b_row[:, :], ALU.add).then_inc(f_add, 1)
                        pool.wait_ge(f_var, at(tb, 1, 1))
                        pool.tensor_tensor(std_b[:, :], std_b[:, :], power[:, 0, :], ALU.pow).then_inc(f_rstd, 1)

            turns(pool, body)


_INS = ["x", "adj", "L0_gnn_Wq", "L0_gnn_Wk", "L0_gnn_Wv", "L0_gnn_bv", "L0_gnn_Wo", "L0_gnn_bo",
        "L1_gnn_W_left", "L1_gnn_W_right", "L1_gnn_W_lin", "L1_gnn_b_lin", "L1_gnn_ln_a", "L1_gnn_ln_b"]
_OUTS = [((32, 256, 384), "float32")]


def kernel(**inputs):
    import numpy as _np
    import concourse.bacc as _bacc
    from concourse import mybir as _mybir
    from concourse.bass_utils import run_bass_kernel_spmd as _run

    nc = _bacc.Bacc("TRN2", target_bir_lowering=False, num_devices=1)
    arrays, args = {}, []
    for name in _INS:
        a = _np.ascontiguousarray(inputs[name])
        arrays[f"in_{name}_dram"] = a
        args.append(nc.dram_tensor(f"in_{name}_dram", a.shape, _mybir.dt.from_np(a.dtype), kind="ExternalInput").ap())
    for i, (shape, dtype) in enumerate(_OUTS):
        dt = _mybir.dt.from_np(_np.dtype(dtype))
        args.append(nc.dram_tensor(f"out_{i}_dram", shape, dt, kind="ExternalOutput").ap())
    adj_resnorm_kernel(nc, *args)
    r = _run(nc, [arrays], core_ids=[0])
    got = tuple(r.results[0][f"out_{i}_dram"] for i in range(len(_OUTS)))
    return got[0]
```

```python
from contextlib import ExitStack

import concourse.bass as bass
from concourse import mybir

P = 128
F32 = mybir.dt.float32
F32R = mybir.dt.float32r
ALU = mybir.AluOpType
ACT = mybir.ActivationFunctionType

LN_EPS = 1e-5
STD_EPS = 1e-3
SUM_EPS = 1e-10


def at(turn, per_turn, k):
    return turn * per_turn + k


def adj_resnorm_kernel(nc, x, adj, Wq, Wk, Wv, bv, Wo, bo, Wl, Wr, Wlin, b_lin, ln_a, ln_b, out):
    B, N, H = x.shape
    LAYERS = Wl.shape[0]
    HEADS = 12
    HD = H // HEADS
    NT = N // P
    HC = H // P
    PER = P // HD
    PAIRS = HEADS // 2
    SCALE = float(H) ** -0.5
    assert (NT, HC, PER, LAYERS) == (2, 3, 4, 2)

    MATS = [Wq, Wk, Wv, Wo] + [w[l] for l in range(LAYERS) for w in (Wl, Wr, Wlin)]
    Q_, K_, V_, O_ = range(4)
    LEFT, RIGHT, LIN = (lambda l: 4 + 3 * l), (lambda l: 5 + 3 * l), (lambda l: 6 + 3 * l)
    BIAS = [bv, bo] + [b_lin[l] for l in range(LAYERS)]
    BV, BO, BL = 0, 1, 2
    VAL = [0, 128, 224, 352]
    SLOT = [VAL[j] - HD * j for j in range(PER)]
    VW = VAL[-1] + HD
    NSTAGE = 5

    with ExitStack() as ctx:
        def sb(name, shape, dt=F32):
            return ctx.enter_context(nc.sbuf_tensor(name, shape, dt))

        def sem(name):
            return ctx.enter_context(nc.semaphore(name))

        w_hi = sb("w_hi", [P, len(MATS), HC, H], F32R)
        w_lo = sb("w_lo", [P, len(MATS), HC, H], F32R)
        ident = sb("ident", [P, P])
        power = sb("power", [P, 2, NT])
        a_col = sb("a_col", [P, HC])
        b_col = sb("b_col", [P, HC])
        a_row = sb("a_row", [P, H])
        b_row = sb("b_row", [P, H])
        xin = sb("xin", [P, NT, H])
        adj_in = sb("adj_in", [P, NT, N])
        xo_hi = sb("xo_hi", [P, HC, N], F32R)
        xo_lo = sb("xo_lo", [P, HC, N], F32R)
        qk_part = sb("qk_part", [P, 2, 4, N], F32R)
        pt_hi = qk_part[:, 0, :, :]
        pt_lo = qk_part[:, 1, :, :]
        stack = sb("stack", [P, 2, HEADS, N], F32R)
        SR = 3 * HD
        v_hi = sb("v_hi", [P, NT, HC, VW], F32R)
        v_lo = sb("v_lo", [P, NT, HC, VW], F32R)
        prob = sb("prob", [P, 2, 2, NT, N])
        junk = sb("junk", [P, NT, N], mybir.dt.bfloat16)
        nmax = sb("nmax", [P, HEADS, NT])
        asum = sb("asum", [P, HEADS, NT])
        esum = sb("esum", [P, HEADS, NT])
        rsum = sb("rsum", [P, HEADS, NT])
        x1 = sb("x1", [P, NT, H])
        stat_a = sb("stat_a", [P, NT, 8])
        rstd_a = sb("rstd_a", [P, NT])
        x1_res = sb("x1_res", [P, NT, H])
        adjT = sb("adjT", [P, NT, N])
        mask = sb("mask", [P, NT, 3 * P])
        h_hi = sb("h_hi", [P, HC, N], F32R)
        h_lo = sb("h_lo", [P, HC, N], F32R)
        m_hi = sb("m_hi", [P, 2 * HC, N], F32R)
        m_lo = sb("m_lo", [P, 2 * HC, N], F32R)
        l_hi = sb("l_hi", [P, NT, H + 2], F32R)
        l_lo = sb("l_lo", [P, NT, H + 2], F32R)
        um = sb("um", [P, NT, 3 * P])
        hT = um[:, :, :].rearrange("p a b -> p (a b)").rearrange("p (c n) -> p c n", c=HC)
        ex = sb("ex", [P, NT, N])
        e_hi = m_hi[:, 0:NT, :]
        e_lo = m_lo[:, 0:NT, :]
        cz = sb("cz", [P, NT, H])
        stat_b = sb("stat_b", [P, NT, 8])
        den = sb("den", [P, NT])
        rden = sb("rden", [P, NT])
        std_b = sb("std_b", [P, NT])
        rstd_b = sb("rstd_b", [P, NT])
        def bias_at(first, second, n):
            return (first, second)[n // 2][0:1].rearrange("p a b -> p (a b)")[:, n % 2 * H:(n % 2 + 1) * H]

        bias_raw = [bias_at(cz[:, :, :], um[:, :, :], n) for n in range(len(BIAS))]
        bias_hi = [bias_at(xo_hi[:, :, :], h_hi[:, :, :], n) for n in range(len(BIAS))]
        bias_lo = [bias_at(xo_lo[:, :, :], h_lo[:, :, :], n) for n in range(len(BIAS))]
        wstage = prob[:, :, :, :, :].rearrange("p a b c d -> p (a b c d)")

        bank = [ctx.enter_context(nc.psum_tensor(f"bank{i}", [P, 512], F32)) for i in range(8)]
        ov_bank = bank[4]
        s_w = [sem(f"weight_landed{i}") for i in range(NSTAGE)]
        s_wt = sem("weight_turned")
        s_whi = sem("weight_hi")
        s_wlo = sem("weight_lo")
        s_id = sem("identity_made")
        s_bias = sem("bias_landed")
        s_bhi = sem("bias_hi")
        s_blo = sem("bias_lo")
        s_brow = sem("bias_rows_placed")
        s_col = sem("ln_vectors_landed")
        s_zero = sem("padding_made")
        s_pow = sem("exponents_made")
        passed = {nc.vector.engine: sem("vector_wait_passed"), nc.gpsimd.engine: sem("gpsimd_wait_passed")}
        x_in = sem("x_landed")
        adj_ld = sem("adj_landed")
        x_res = sem("x_residual_landed")
        xt_full = sem("xt_in_psum")
        xt_hi = sem("xt_hi_done")
        xt_lo = sem("xt_lo_done")
        qk_full = sem("qk_in_psum")
        qk_hi = sem("qk_hi_done")
        qk_lo = sem("qk_lo_done")
        stacked = [sem(f"stacked{g}") for g in range(PAIRS)]
        v_full = sem("v_in_psum")
        v_hi_s = sem("v_hi_done")
        v_lo_s = sem("v_lo_done")
        s_full = sem("scores_in_psum")
        s_neg = sem("scores_negated")
        s_abs = sem("scores_abs_summed")
        s_exp = sem("exp_done")
        s_rec = sem("esum_inverted")
        s_nz = sem("zero_rows_found")
        s_rn = sem("row_factor_ready")
        s_norm = sem("probs_normalised")
        pt_full = sem("pt_in_psum")
        pt_hi_s = sem("pt_hi_done")
        pt_lo_s = sem("pt_lo_done")
        pv_used = sem("pv_products_done")
        ot_full = sem("heads_out_in_psum")
        ot_hi = sem("heads_out_hi_done")
        ot_lo = sem("heads_out_lo_done")
        o_full = sem("o_in_psum")
        o_sum = sem("residual_added")
        a_stat = sem("x1_stats")
        a_aggr = sem("x1_stats_joined")
        a_var = sem("x1_var_ready")
        a_rstd = sem("x1_rstd")
        x1_ready = sem("x1_ready")
        at_full = sem("adjt_in_psum")
        at_done = sem("adjt_copied")
        masks = sem("masks_made")
        res_kept = sem("x1_residual_kept")
        t_full = sem("ht_in_psum")
        h_f32 = sem("ht_relu_done")
        h_hi_s = sem("h_hi_done")
        h_lo_s = sem("h_lo_done")
        m_full = sem("m_in_psum")
        m_hi_s = sem("m_hi_done")
        m_lo_s = sem("m_lo_done")
        l_full = sem("hlin_in_psum")
        l_hi_s = sem("hlin_hi_done")
        l_lo_s = sem("hlin_lo_done")
        u_full = sem("u_in_psum")
        u_mask = sem("u_masked")
        u_add = sem("u_halves_added")
        u_exp = sem("u_exp_done")
        u_adj = sem("u_exp_times_adj")
        e_hi_s = sem("e_hi_done")
        e_lo_s = sem("e_lo_done")
        c_full = sem("ctx_in_psum")
        c_den = sem("ctx_den_ready")
        c_rden = sem("ctx_rden_ready")
        c_copy = sem("ctx_scaled")
        b_stat = sem("ctx_stats")
        b_aggr = sem("ctx_stats_joined")
        b_var = sem("ctx_var_ready")
        b_std = sem("ctx_std")
        b_stde = sem("ctx_std_plus_eps")
        b_rstd = sem("ctx_rstd")
        z_ready = sem("ctx_normalised")
        f_mul = sem("final_scaled")
        f_add = sem("final_shifted")
        f_res = sem("final_residual_added")
        f_stat = sem("final_stats")
        f_aggr = sem("final_stats_joined")
        f_var = sem("final_var_ready")
        f_rstd = sem("final_rstd")
        f_out = sem("final_ready")
        stored = sem("out_stored")

        A_STEPS = {"XT", "QK", "V", "S", "N", "T", "PV", "AT", "O", "LN"}
        B_STEPS = {"keep", "ht", "m", "lin", "u", "e", "ctx", "z"}
        C_STEPS = {"zc", "affine", "residual", "store"}
        ORDERS = {
            "sp": [
                ("XT",), ("QK", 0), ("QK", 1), ("QK", 2), ("store",), ("V",), ("AT",),
            ],
            "pe": [
                ("XT",), ("ht", 0), ("QK", 0), ("m", 0, 0), ("QK", 1), ("m", 0, 1), ("QK", 2), ("m", 0, 2),
                ("S", 0), ("V",), ("S", 1), ("u", 0), ("T", 0), ("S", 2), ("lin", 0), ("S", 3), ("PV", 0),
                ("T", 1), ("ctx", 0), ("PV", 1), ("S", 4), ("T", 2), ("ht", 1), ("PV", 2), ("S", 5),
                ("m", 1, 0), ("T", 3), ("m", 1, 1), ("m", 1, 2), ("PV", 3), ("T", 4), ("lin", 1), ("PV", 4),
                ("T", 5), ("u", 1), ("PV", 5), ("O",), ("AT",), ("ctx", 1),
            ],
            "act": [
                ("XT",), ("ht", 0), ("QK", 0), ("m", 0, 0), ("QK", 1), ("m", 0, 1), ("m", 0, 2), ("QK", 2),
                ("S", 0), ("V",), ("S", 1), ("u", 0), ("e", 0), ("S", 2), ("T", 0), ("lin", 0), ("T", 1),
                ("ctx", 0), ("PV", 1), ("S", 3), ("T", 2), ("ht", 1), ("S", 4), ("T", 3), ("m", 1, 0), ("S", 5),
                ("PV", 3), ("m", 1, 1), ("T", 4), ("m", 1, 2), ("T", 5), ("lin", 1), ("PV", 5), ("u", 1),
                ("e", 1), ("AT",), ("ctx", 1),
            ],
            "dve": [
                ("XT",), ("ht", 0), ("QK", 0), ("zc",), ("m", 0, 0), ("QK", 1), ("m", 0, 1), ("residual",),
                ("S", 0), ("m", 0, 2), ("QK", 2), ("S", 1), ("N", 0), ("u", 0), ("V",), ("S", 2), ("e", 0),
                ("N", 1), ("store",), ("T", 0), ("lin", 0), ("N", 2), ("T", 1), ("ctx", 0), ("S", 3), ("z", 0),
                ("PV", 1), ("T", 2), ("S", 4), ("ht", 1), ("N", 3), ("S", 5), ("N", 4), ("T", 3), ("m", 1, 0),
                ("PV", 3), ("m", 1, 1), ("N", 5), ("T", 4), ("m", 1, 2), ("lin", 1), ("T", 5), ("u", 1),
                ("PV", 5), ("e", 1), ("O",), ("ctx", 1), ("LN",),
            ],
            "pool": [
                ("zc",), ("affine",), ("e", 0), ("residual",), ("keep",), ("z", 0), ("e", 1), ("O",), ("AT",),
            ],
        }

        HELD = {"ht": ("T0", "T1"), "lin": ("L0", "L1"), "u": ("U0", "U1"), "ctx": ("C0", "C1")}
        UNITS = [(l[0], u) for name, *l in ORDERS["pe"] if name in B_STEPS
                 for u in ([f"M{l[1]}"] if name == "m" else HELD.get(name, ()))]
        LAST = {"T0": (h_lo_s, 4, 1), "T1": (h_lo_s, 4, 2), "M0": (m_lo_s, 6, 1), "M1": (m_lo_s, 6, 2),
                "M2": (m_lo_s, 6, 3), "L0": (l_lo_s, 4, 1), "L1": (l_lo_s, 4, 2), "U0": (u_mask, 4, 1),
                "U1": (u_mask, 4, 2), "C0": (c_copy, 4, 1), "C1": (c_copy, 4, 2)}

        def b_bank(l, u):
            return bank[5 + UNITS.index((l, u)) % 3]

        def b_bank_free(pe, l, u, tb, first):
            i = UNITS.index((l, u))
            before = [k for k in range(len(UNITS)) if k % 3 == i % 3]
            n = before.index(i)
            pl, pu = UNITS[before[n - 1]]
            s, per, k = LAST[pu]
            if n > 0:
                pe.wait_ge(s, at(tb, per, pl * per // LAYERS + k))
            elif not first:
                pe.wait_ge(s, at(tb - 1, per, pl * per // LAYERS + k))

        def r32(ap):
            return ap.bitcast(F32)

        def v_view(v, n, a):
            o = VAL[2 * a]
            return v[:, n, :, o:o + 160].rearrange("p c (j w) -> p c j w", w=32)[:, :, 0:5:4, :]

        def v_src(n, a):
            return bank[2 + n][:, 0:H].rearrange("p (c j w) -> p c j w", c=HC, w=HD)[:, :, 2 * a:2 * a + 2, :]

        def steps(eng, ta, tb, tc):
            for name, *arg in ORDERS[eng]:
                t = ta if name in A_STEPS else tb if name in B_STEPS else tc
                if t is not None:
                    yield name, arg

        def turns(eng, body):
            body(0, None, None, True, True, True)
            body(1, 0, None, False, True, True)
            with eng.Fori(2, B - 1) as t:
                body(t, t - 1, t - 2, False, False, True)
            body(B - 1, B - 2, B - 3, False, False, False)
            body(None, B - 1, B - 2, False, False, False)
            body(None, None, B - 1, False, False, False)

        def wait_apart(eng, s, value):
            eng.wait_ge(s, value)
            eng.sem_inc(passed[eng.engine], 1)

        block = ctx.enter_context(nc.Block())

        @block.sync
        def _(sp):
            def load_x(t):
                sp.dma_start(xin[:, :, :], x[t, :, :].rearrange("(n p) h -> p n h", p=P)).then_inc(x_in, 16)

            def load_adj(t):
                sp.dma_start(adj_in[:, :, :], adj[t, :, :].rearrange("(n p) m -> p n m", p=P)).then_inc(adj_ld, 16)

            for i in range(len(MATS) * HC):
                if i >= NSTAGE:
                    sp.wait_ge(s_wt, i - NSTAGE + 1)
                sp.dma_start(wstage[:, i % NSTAGE * H:(i % NSTAGE + 1) * H],
                             MATS[i // HC][i % HC * P:(i % HC + 1) * P, :]).then_inc(s_w[i % NSTAGE], 16)
                if i == 2:
                    load_x(0)
                    load_adj(0)
                if i == NSTAGE - 1:
                    for n, b in enumerate(BIAS):
                        sp.dma_start(bias_raw[n], b.rearrange("(a h) -> a h", a=1)).then_inc(s_bias, 16)
                    sp.dma_start(a_col[:, :], ln_a[0, :].rearrange("(c p) -> p c", p=P),
                                 allow_slow_non_contiguous=True).then_inc(s_col, 16)
                    sp.dma_start(b_col[:, :], ln_b[0, :].rearrange("(c p) -> p c", p=P),
                                 allow_slow_non_contiguous=True).then_inc(s_col, 16)
                    sp.dma_start(a_row[:, :], ln_a[1, :].partition_broadcast(P)).then_inc(s_col, 16)
                    sp.dma_start(b_row[:, :], ln_b[1, :].partition_broadcast(P)).then_inc(s_col, 16)
            sp.wait_ge(s_blo, len(BIAS))
            for n in range(len(BIAS)):
                for part, row in ((bias_hi, SR), (bias_lo, SR + 1)):
                    sp.dma_start(r32(stack[row:row + 1, 0, 2 * n:2 * n + 2, :].rearrange("p a b -> p (a b)")[:, 0:H]),
                                 r32(part[n])).then_inc(s_brow, 16)

            def body(ta, tb, tc, first_a, first_b, more):
                for name, arg in steps("sp", ta, tb, tc):
                    if name == "XT" and more:
                        sp.wait_ge(xt_full, at(ta, 2, 2))
                        load_x(ta + 1)
                    if name == "QK":
                        c, = arg
                        sp.wait_ge(qk_lo, at(ta, HC, c + 1))
                        part = qk_part[:, c % 2, :, :]
                        for j in range(PER):
                            src = part[HD * j:HD * (j + 1), :, :]
                            h = PER * c + j
                            for r, (a, step) in enumerate(((0, 2), (0, 3), (1, 1))):
                                sp.dma_start(r32(stack[HD * r:HD * (r + 1), :, h, :]),
                                             r32(src[:, a:a + step + 1:step, :])).then_inc(stacked[h // 2], 16)
                    if name == "V":
                        if not first_a:
                            sp.wait_ge(res_kept, at(ta - 1, 1, 1))
                        sp.dma_start(x1[:, :, :], x[ta, :, :].rearrange("(n p) h -> p n h", p=P)).then_inc(x_res, 16)
                    if name == "AT" and more:
                        sp.wait_ge(masks, at(ta, 1, 1))
                        load_adj(ta + 1)
                    if name == "store":
                        sp.wait_ge(f_out, at(tc, 2, 2))
                        sp.dma_start(out[tc, :, :].rearrange("(n p) h -> p n h", p=P), cz[:, :, :]).then_inc(stored, 16)

            turns(sp, body)
            sp.wait_ge(stored, 16 * B)

        @block.tensor
        def _(pe):
            def mm3(o, lh, ll, rh, rl, start, stop):
                pe.matmul(o, lh, rh, start=start, stop=False)
                pe.matmul(o, lh, rl, start=False, stop=False)
                return pe.matmul(o, ll, rh, start=False, stop=stop)

            def bias(o, n, start):
                return pe.matmul(o, stack[SR:SR + 2, 1, 0, 0:P],
                                 stack[SR:SR + 2, 0, 2 * n:2 * n + 2, :].rearrange("p a b -> p (a b)")[:, 0:H],
                                 start=start, stop=False)

            pe.wait_ge(s_id, 2)
            for i in range(len(MATS) * HC):
                pe.wait_ge(s_w[i % NSTAGE], 16 * (i // NSTAGE + 1))
                if i >= 4:
                    pe.wait_ge(s_wlo, i - 3)
                for c in range(HC):
                    o = i % NSTAGE * H + c * P
                    mm = pe.transpose(bank[i % 4][:, c * P:(c + 1) * P], wstage[:, o:o + P], ident[:, :])
                mm.then_inc(s_wt, 1)
            pe.wait_ge(s_wlo, len(MATS) * HC)
            pe.wait_ge(s_brow, 16 * 2 * len(BIAS))
            pe.wait_ge(s_zero, 5)

            def body(ta, tb, tc, first_a, first_b, more):
                for name, arg in steps("pe", ta, tb, tc):
                    if name == "XT":
                        pe.wait_ge(x_in, at(ta, 16, 16))
                        for u, cs in enumerate(((0, 1), (2,))):
                            if not first_a:
                                pe.wait_ge(o_sum, at(ta - 1, 2, u + 1))
                            for c in cs:
                                for n in range(NT):
                                    mm = pe.transpose(bank[u][:, (c % 2) * N + n * P:(c % 2) * N + (n + 1) * P],
                                                      xin[:, n, c * P:(c + 1) * P], ident[:, :])
                            mm.then_inc(xt_full, 1)
                    if name == "QK":
                        m, = arg
                        if m == 0:
                            if not first_a:
                                pe.wait_ge(at_done, at(ta - 1, 1, 1))
                            pe.wait_ge(xt_lo, at(ta, 2, 2))
                        if m == 1 and not first_a:
                            pe.wait_ge(pt_lo_s, at(ta - 1, HEADS, HEADS))
                        if m == 2 and not first_a:
                            pe.wait_ge(ot_lo, at(ta - 1, HC, HC))
                        b = bank[2 + m]
                        for half, w in enumerate((Q_, K_)):
                            for c in range(HC):
                                mm = mm3(b[:, half * N:(half + 1) * N],
                                         w_hi[:, w, c, m * P:(m + 1) * P], w_lo[:, w, c, m * P:(m + 1) * P],
                                         xo_hi[:, c, :], xo_lo[:, c, :], c == 0, c == HC - 1)
                        mm.then_inc(qk_full, 1)
                    if name == "V":
                        for n in range(NT):
                            pe.wait_ge(qk_lo, at(ta, HC, n + 1))
                            o = bank[2 + n][:, 0:H]
                            bias(o, BV, True)
                            for c in range(HC):
                                mm = mm3(o, xo_hi[:, c, n * P:(n + 1) * P], xo_lo[:, c, n * P:(n + 1) * P],
                                         w_hi[:, V_, c, :], w_lo[:, V_, c, :], False, c == HC - 1)
                            mm.then_inc(v_full, 1)
                    if name == "S":
                        for h in (2 * arg[0], 2 * arg[0] + 1):
                            if h % 2 == 0:
                                pe.wait_ge(stacked[h // 2], at(ta, 16 * 6, 16 * 6))
                            if h >= 2:
                                pe.wait_ge(s_neg, at(ta, 2 * HEADS, 2 * (h - 1)))
                            for n in range(NT):
                                mm = pe.matmul(bank[h % 2][:, n * N:(n + 1) * N],
                                               stack[0:SR, 0, h, n * P:(n + 1) * P], stack[0:SR, 1, h, :],
                                               start=True, stop=True)
                            mm.then_inc(s_full, 1)
                    if name == "T":
                        g, = arg
                        pe.wait_ge(s_norm, at(ta, PAIRS, g + 1))
                        for i in range(2):
                            h = 2 * g + i
                            if g == 0:
                                pe.wait_ge(v_lo_s, at(ta, 2 * NT, 2 * i + 2))
                            else:
                                pe.wait_ge(pt_lo_s, at(ta, HEADS, h - 1))
                            for kt in range(NT):
                                for n in range(NT):
                                    mm = pe.transpose(bank[2 + i][:, kt * N + n * P:kt * N + (n + 1) * P],
                                                      prob[:, g % 2, i, n, kt * P:(kt + 1) * P], ident[:, :])
                            mm.then_inc(pt_full, 1)
                    if name == "PV":
                        g, = arg
                        c = g // 2
                        if g % 2 == 0:
                            if c > 0:
                                pe.wait_ge(ot_lo, at(ta, HC, c))
                            else:
                                pe.wait_ge(qk_lo, at(ta, HC, HC))
                        for i in range(2):
                            j = 2 * (g % 2) + i
                            pe.wait_ge(pt_lo_s, at(ta, HEADS, 2 * g + i + 1))
                            for kt in range(NT):
                                sl = slice(SLOT[j], SLOT[j] + P)
                                mm = mm3(ov_bank[:, 0:N], v_hi[:, kt, c, sl], v_lo[:, kt, c, sl],
                                         pt_hi[:, 2 * i + kt, :], pt_lo[:, 2 * i + kt, :],
                                         j == 0 and kt == 0, j == PER - 1 and kt == NT - 1)
                        mm.then_inc(pv_used, 1)
                    if name == "AT":
                        pe.wait_ge(pt_lo_s, at(ta, HEADS, HEADS - 1))
                        for J in range(NT):
                            for n in range(NT):
                                mm = pe.transpose(bank[2][:, J * N + n * P:J * N + (n + 1) * P],
                                                  adj_in[:, n, J * P:(J + 1) * P], ident[:, :])
                        mm.then_inc(at_full, 1)
                    if name == "O":
                        pe.wait_ge(s_neg, at(ta, 2 * HEADS, 2 * HEADS))
                        pe.wait_ge(ot_lo, at(ta, HC, HC))
                        for n in range(NT):
                            o = bank[n][:, 0:H]
                            bias(o, BO, True)
                            for c in range(HC):
                                mm = mm3(o, xo_hi[:, c, n * P:(n + 1) * P], xo_lo[:, c, n * P:(n + 1) * P],
                                         w_hi[:, O_, c, :], w_lo[:, O_, c, :], False, c == HC - 1)
                            mm.then_inc(o_full, 1)
                    if name == "ht":
                        l, = arg
                        src = x1 if l == 0 else cz
                        if l == 0:
                            pe.wait_ge(x1_ready, at(tb, NT, NT))
                        else:
                            pe.wait_ge(z_ready, at(tb, 4, 2))
                        for u, cs in enumerate(((0, 1), (2,))):
                            b_bank_free(pe, l, f"T{u}", tb, first_b)
                            b = b_bank(l, f"T{u}")
                            for c in cs:
                                for n in range(NT):
                                    mm = pe.transpose(b[:, (c % 2) * N + n * P:(c % 2) * N + (n + 1) * P],
                                                      src[:, n, c * P:(c + 1) * P], ident[:, :])
                            mm.then_inc(t_full, 1)
                    if name == "m":
                        l, u = arg
                        b_bank_free(pe, l, f"M{u}", tb, first_b)
                        if u == 0:
                            pe.wait_ge(h_lo_s, at(tb, 4, 2 * l + 2))
                        b = b_bank(l, f"M{u}")
                        for half in range(2):
                            k = 2 * u + half
                            w, m = (LEFT(l), k) if k < HC else (RIGHT(l), k - HC)
                            for c in range(HC):
                                mm = mm3(b[:, half * N:(half + 1) * N],
                                         w_hi[:, w, c, m * P:(m + 1) * P], w_lo[:, w, c, m * P:(m + 1) * P],
                                         h_hi[:, c, :], h_lo[:, c, :], c == 0, c == HC - 1)
                        mm.then_inc(m_full, 1)
                    if name == "lin":
                        l, = arg
                        for n in range(NT):
                            b_bank_free(pe, l, f"L{n}", tb, first_b)
                            o = b_bank(l, f"L{n}")[:, 0:H]
                            bias(o, BL + l, True)
                            for c in range(HC):
                                mm = mm3(o, h_hi[:, c, n * P:(n + 1) * P], h_lo[:, c, n * P:(n + 1) * P],
                                         w_hi[:, LIN(l), c, :], w_lo[:, LIN(l), c, :], False, c == HC - 1)
                            mm.then_inc(l_full, 1)
                    if name == "u":
                        l, = arg
                        pe.wait_ge(m_lo_s, at(tb, 6, 3 * l + 3))
                        for J in range(NT):
                            b_bank_free(pe, l, f"U{J}", tb, first_b)
                            b = b_bank(l, f"U{J}")
                            js = slice(J * P, (J + 1) * P)
                            for side, lo, hi, to in ((0, 0, (J + 1) * P, 0), (1, J * P, N, (J + 1) * P)):
                                for c in range(HC):
                                    mm = mm3(b[:, to:to + hi - lo], m_hi[:, side * HC + c, js],
                                             m_lo[:, side * HC + c, js], h_hi[:, c, lo:hi], h_lo[:, c, lo:hi],
                                             c == 0, c == HC - 1)
                            mm.then_inc(u_full, 1)
                    if name == "ctx":
                        l, = arg
                        pe.wait_ge(e_lo_s, at(tb, 2, l + 1))
                        pe.wait_ge(l_lo_s, at(tb, 4, 2 * l + 2))
                        for n in range(NT):
                            b_bank_free(pe, l, f"C{n}", tb, first_b)
                            b = b_bank(l, f"C{n}")
                            for J in range(NT):
                                mm = mm3(b[:, 0:H + 2], e_hi[:, J, n * P:(n + 1) * P], e_lo[:, J, n * P:(n + 1) * P],
                                         l_hi[:, J, :], l_lo[:, J, :], J == 0, J == NT - 1)
                            mm.then_inc(c_full, 1)

            turns(pe, body)

        @block.scalar
        def _(act):
            for i in range(len(MATS) * HC):
                act.wait_ge(s_wt, i + 1)
                act.activation(w_hi[:, i // HC, :, i % HC * P:(i % HC + 1) * P],
                               bank[i % 4][:, 0:H].rearrange("p (c o) -> p c o", c=HC), ACT.Copy,
                               scale=0.5 * SCALE if i // HC == Q_ else 1.0).then_inc(s_whi, 1)

            def body(ta, tb, tc, first_a, first_b, more):
                for name, arg in steps("act", ta, tb, tc):
                    if name == "XT":
                        if not first_a:
                            act.wait_ge(o_full, at(ta - 1, NT, NT))
                        for u, w in enumerate((2, 1)):
                            act.wait_ge(xt_full, at(ta, 2, u + 1))
                            act.activation(xo_hi[:, 2 * u:2 * u + w, :],
                                           bank[u][:, 0:w * N].rearrange("p (c n) -> p c n", c=w),
                                           ACT.Copy).then_inc(xt_hi, 1)
                    if name == "QK":
                        m, = arg
                        act.wait_ge(qk_full, at(ta, HC, m + 1))
                        if m == 0 and not first_a:
                            act.wait_ge(pv_used, at(ta - 1, PAIRS, PAIRS))
                        if m == 2:
                            act.wait_ge(stacked[0], at(ta, 16 * 6, 16 * 6))
                            act.wait_ge(stacked[1], at(ta, 16 * 6, 16 * 6))
                        act.activation(qk_part[:, m % 2, 0:3:2, :],
                                       bank[2 + m][:, :].rearrange("p (a n) -> p a n", a=2),
                                       ACT.Copy).then_inc(qk_hi, 1)
                    if name == "V":
                        if not first_a:
                            act.wait_ge(pv_used, at(ta - 1, PAIRS, PAIRS))
                        for n in range(NT):
                            act.wait_ge(v_full, at(ta, NT, n + 1))
                            for a in range(2):
                                act.activation(v_view(v_hi, n, a), v_src(n, a), ACT.Copy).then_inc(v_hi_s, 1)
                    if name == "S":
                        g, = arg
                        for h in (2 * g, 2 * g + 1):
                            for n in range(NT):
                                k = 2 * h + n
                                act.wait_ge(s_neg, at(ta, 2 * HEADS, k + 1))
                                if k >= 2:
                                    act.wait_ge(s_abs, at(ta, 2 * HEADS, k - 1))
                                elif not first_a:
                                    act.wait_ge(s_abs, at(ta - 1, 2 * HEADS, 2 * HEADS + k - 1))
                                act.activation(junk[:, n, :], prob[:, g % 2, h % 2, n, :], ACT.Abs,
                                               accum_out=asum[:, h, n:n + 1]).then_inc(s_abs, 1)
                            for n in range(NT):
                                p = prob[:, g % 2, h % 2, n, :]
                                act.wait_ge(s_abs, at(ta, 2 * HEADS, 2 * h + n + 1))
                                act.activation(p, p, ACT.Exp, bias=nmax[:, h, n:n + 1], scale=-1.0,
                                               accum_out=esum[:, h, n:n + 1]).then_inc(s_exp, 1)
                    if name == "T":
                        g, = arg
                        if g > 0:
                            act.wait_ge(pv_used, at(ta, PAIRS, g))
                        else:
                            for k in range(2, PAIRS):
                                act.wait_ge(stacked[k], at(ta, 16 * 6, 16 * 6))
                        for i in range(2):
                            act.wait_ge(pt_full, at(ta, HEADS, 2 * g + i + 1))
                            act.activation(pt_hi[:, 2 * i:2 * i + 2, :],
                                           bank[2 + i][:, :].rearrange("p (k n) -> p k n", k=NT),
                                           ACT.Copy).then_inc(pt_hi_s, 1)
                    if name == "PV" and arg[0] % 2 == 1:
                        c = arg[0] // 2
                        act.wait_ge(pv_used, at(ta, PAIRS, arg[0] + 1))
                        if c == 0:
                            act.wait_ge(v_full, at(ta, NT, NT))
                        act.activation(xo_hi[:, c, :], ov_bank[:, 0:N], ACT.Copy).then_inc(ot_hi, 1)
                    if name == "AT":
                        act.wait_ge(at_full, at(ta, 1, 1))
                        if not first_a:
                            act.wait_ge(u_adj, at(ta - 1, LAYERS, LAYERS))
                        act.activation(adjT[:, :, :], bank[2][:, :].rearrange("p (k n) -> p k n", k=NT),
                                       ACT.Copy).then_inc(at_done, 1)
                    if name == "ht":
                        l, = arg
                        for u, w in enumerate((2, 1)):
                            act.wait_ge(t_full, at(tb, 4, 2 * l + u + 1))
                            b = b_bank(l, f"T{u}")
                            if l == 0:
                                if u == 0 and not first_b:
                                    act.wait_ge(u_full, at(tb - 1, 4, 4))
                                    act.wait_ge(l_full, at(tb - 1, 4, 4))
                                act.activation(h_hi[:, 2 * u:2 * u + w, :],
                                               b[:, 0:w * N].rearrange("p (c n) -> p c n", c=w),
                                               ACT.Copy).then_inc(h_hi_s, 1)
                            else:
                                for c in range(2 * u, 2 * u + w):
                                    if c == 0:
                                        act.wait_ge(s_col, 64)
                                        act.wait_ge(u_exp, at(tb, 4, 2))
                                    act.activation(hT[:, c, :], b[:, (c % 2) * N:(c % 2 + 1) * N], ACT.Relu,
                                                   scale=a_col[:, c:c + 1],
                                                   bias=b_col[:, c:c + 1]).then_inc(h_f32, 1)
                    if name == "m":
                        l, u = arg
                        act.wait_ge(m_full, at(tb, 6, 3 * l + u + 1))
                        if u == 0 and (l > 0 or not first_b):
                            act.wait_ge(c_full, at(tb, 4, 2) if l > 0 else at(tb - 1, 4, 4))
                        act.activation(m_hi[:, 2 * u:2 * u + 2, :],
                                       b_bank(l, f"M{u}")[:, :].rearrange("p (c n) -> p c n", c=2),
                                       ACT.Copy).then_inc(m_hi_s, 1)
                    if name == "lin":
                        l, = arg
                        if l > 0 or not first_b:
                            act.wait_ge(c_full, at(tb, 4, 2) if l > 0 else at(tb - 1, 4, 4))
                        for n in range(NT):
                            act.wait_ge(l_full, at(tb, 4, 2 * l + n + 1))
                            act.activation(l_hi[:, n, 0:H], b_bank(l, f"L{n}")[:, 0:H],
                                           ACT.Copy).then_inc(l_hi_s, 1)
                    if name == "u":
                        l, = arg
                        for J in range(NT):
                            act.wait_ge(u_add, at(tb, 4, 2 * l + J + 1))
                            if J == 0 and (l > 0 or not first_b):
                                act.wait_ge(e_lo_s, at(tb, 2, 1) if l > 0 else at(tb - 1, 2, 2))
                            act.activation(ex[:, J, :], um[:, J, (1 - J) * P:(1 - J) * P + N], ACT.Exp,
                                           scale=SCALE).then_inc(u_exp, 1)
                    if name == "e":
                        l, = arg
                        act.wait_ge(u_adj, at(tb, LAYERS, l + 1))
                        act.wait_ge(u_full, at(tb, 4, 2 * l + 2))
                        act.activation(e_hi, ex[:, :, :], ACT.Copy).then_inc(e_hi_s, 1)
                    if name == "ctx":
                        l, = arg
                        if l == 0 and not first_b:
                            act.wait_ge(stored, at(tb - 1, 16, 16))
                        if l == 1:
                            act.wait_ge(t_full, at(tb, 4, 4))
                        for n in range(NT):
                            act.wait_ge(c_rden, at(tb, 4, 2 * l + n + 1))
                            act.activation(cz[:, n, :], b_bank(l, f"C{n}")[:, 0:H], ACT.Copy,
                                           scale=rden[:, n:n + 1]).then_inc(c_copy, 1)

            turns(act, body)

        @block.vector
        def _(dve):
            def normalise(t, l):
                for n in range(NT):
                    dve.wait_ge(c_copy, at(t, 4, 2 * l + n + 1))
                    dve.bn_stats(stat_b[:, n, 0:6], cz[:, n, :]).then_inc(b_stat, 1)
                wait_apart(dve, b_stat, at(t, 4, 2 * l + 2))
                for n in range(NT):
                    dve.bn_aggr(stat_b[:, n, 6:8], stat_b[:, n, 0:6]).then_inc(b_aggr, 1)
                dve.wait_ge(b_aggr, at(t, 4, 2 * l + 2))
                dve.tensor_scalar(std_b[:, :], stat_b[:, :, 7], H / (H - 1.0), None, ALU.mult).then_inc(b_var, 1)
                dve.wait_ge(b_std, at(t, 2, l + 1))
                dve.tensor_scalar(std_b[:, :], std_b[:, :], STD_EPS, None, ALU.add).then_inc(b_stde, 1)
                dve.wait_ge(b_stde, at(t, 2, l + 1))
                dve.reciprocal(rstd_b[:, :], std_b[:, :]).then_inc(b_rstd, 1)
                dve.wait_ge(b_rstd, at(t, 2, l + 1))
                for n in range(NT):
                    dve.tensor_scalar(cz[:, n, :], cz[:, n, :], stat_b[:, n, 6:7], rstd_b[:, n:n + 1],
                                      ALU.subtract, ALU.mult).then_inc(z_ready, 1)

            dve.memset(r32(stack[SR:P, 1, 0, 0:P]), 1.0).then_inc(s_zero, 1)
            dve.wait_ge(s_bias, 16 * len(BIAS))
            for n in range(len(BIAS)):
                dve.tensor_copy(bias_hi[n], bias_raw[n]).then_inc(s_bhi, 1)
            dve.wait_ge(s_bhi, len(BIAS))
            for n in range(len(BIAS)):
                dve.tensor_tensor(bias_lo[n], bias_raw[n], r32(bias_hi[n]), ALU.subtract).then_inc(s_blo, 1)
            for i in range(len(MATS) * HC):
                dst = slice(i % HC * P, (i % HC + 1) * P)
                dve.wait_ge(s_whi, i + 1)
                dve.scalar_tensor_tensor(out=w_lo[:, i // HC, :, dst],
                                         in0=bank[i % 4][:, 0:H].rearrange("p (c o) -> p c o", c=HC),
                                         scalar=0.5 * SCALE if i // HC == Q_ else 1.0,
                                         in1=r32(w_hi[:, i // HC, :, dst]),
                                         op0=ALU.mult, op1=ALU.subtract).then_inc(s_wlo, 1)

            def body(ta, tb, tc, first_a, first_b, more):
                for name, arg in steps("dve", ta, tb, tc):
                    if name == "XT":
                        for u, w in enumerate((2, 1)):
                            dve.wait_ge(xt_hi, at(ta, 2, u + 1))
                            dve.tensor_tensor(xo_lo[:, 2 * u:2 * u + w, :],
                                              bank[u][:, 0:w * N].rearrange("p (c n) -> p c n", c=w),
                                              r32(xo_hi[:, 2 * u:2 * u + w, :]), ALU.subtract).then_inc(xt_lo, 1)
                    if name == "QK":
                        m, = arg
                        dve.wait_ge(qk_hi, at(ta, HC, m + 1))
                        dve.tensor_tensor(qk_part[:, m % 2, 1:4:2, :],
                                          bank[2 + m][:, :].rearrange("p (a n) -> p a n", a=2),
                                          r32(qk_part[:, m % 2, 0:3:2, :]), ALU.subtract).then_inc(qk_lo, 1)
                    if name == "V":
                        for n in range(NT):
                            dve.wait_ge(v_hi_s, at(ta, 2 * NT, 2 * n + 2))
                            for a in range(2):
                                dve.tensor_tensor(v_view(v_lo, n, a), v_src(n, a), r32(v_view(v_hi, n, a)),
                                                  ALU.subtract).then_inc(v_lo_s, 1)
                    if name == "S":
                        g, = arg
                        if g == 0:
                            dve.wait_ge(adj_ld, at(ta, 16, 16))
                            if not first_a:
                                dve.wait_ge(pt_full, at(ta - 1, HEADS, HEADS))
                        elif g >= 2:
                            dve.wait_ge(pt_full, at(ta, HEADS, 2 * g - 2))
                        for i in range(2):
                            h = 2 * g + i
                            wait_apart(dve, s_full, at(ta, HEADS, h + 1))
                            for n in range(NT):
                                dve.tensor_tensor_reduce(prob[:, g % 2, i, n, :], bank[h % 2][:, n * N:(n + 1) * N],
                                                         adj_in[:, n, :], -2.0, 3.0e38, ALU.add, ALU.min,
                                                         nmax[:, h, n:n + 1]).then_inc(s_neg, 1)
                    if name == "N":
                        g, = arg
                        hs = slice(2 * g, 2 * g + 2)
                        dve.wait_ge(s_exp, at(ta, 2 * HEADS, 4 * g + 4))
                        dve.reciprocal(rsum[:, hs, :], esum[:, hs, :]).then_inc(s_rec, 1)
                        dve.wait_ge(s_rec, at(ta, PAIRS, g + 1))
                        dve.scalar_tensor_tensor(out=rsum[:, hs, :], in0=asum[:, hs, :], scalar=0.0,
                                                 in1=rsum[:, hs, :], op0=ALU.not_equal,
                                                 op1=ALU.mult).then_inc(s_rn, 1)
                        dve.wait_ge(s_rn, at(ta, PAIRS, g + 1))
                        for i in range(2):
                            for n in range(NT):
                                p = prob[:, g % 2, i, n, :]
                                ins = dve.tensor_scalar(p, p, rsum[:, 2 * g + i, n:n + 1], None, ALU.mult)
                        ins.then_inc(s_norm, 1)
                    if name == "T":
                        g, = arg
                        for i in range(2):
                            dve.wait_ge(pt_hi_s, at(ta, HEADS, 2 * g + i + 1))
                            dve.tensor_tensor(pt_lo[:, 2 * i:2 * i + 2, :],
                                              bank[2 + i][:, :].rearrange("p (k n) -> p k n", k=NT),
                                              r32(pt_hi[:, 2 * i:2 * i + 2, :]), ALU.subtract).then_inc(pt_lo_s, 1)
                    if name == "PV" and arg[0] % 2 == 1:
                        c = arg[0] // 2
                        dve.wait_ge(ot_hi, at(ta, HC, c + 1))
                        dve.tensor_tensor(xo_lo[:, c, :], ov_bank[:, 0:N], r32(xo_hi[:, c, :]),
                                          ALU.subtract).then_inc(ot_lo, 1)
                    if name == "O":
                        dve.wait_ge(x_res, at(ta, 16, 16))
                        for n in range(NT):
                            dve.wait_ge(o_full, at(ta, NT, n + 1))
                            dve.tensor_tensor(x1[:, n, :], bank[n][:, 0:H], x1[:, n, :], ALU.add).then_inc(o_sum, 1)
                        for n in range(NT):
                            dve.wait_ge(o_sum, at(ta, NT, n + 1))
                            dve.bn_stats(stat_a[:, n, 0:6], x1[:, n, :]).then_inc(a_stat, 1)
                        wait_apart(dve, a_stat, at(ta, NT, NT))
                        for n in range(NT):
                            dve.bn_aggr(stat_a[:, n, 6:8], stat_a[:, n, 0:6]).then_inc(a_aggr, 1)
                        dve.wait_ge(a_aggr, at(ta, NT, NT))
                        dve.tensor_scalar(rstd_a[:, :], stat_a[:, :, 7], LN_EPS, None,
                                          ALU.add).then_inc(a_var, 1)
                    if name == "LN":
                        dve.wait_ge(a_rstd, at(ta, 1, 1))
                        for n in range(NT):
                            dve.tensor_scalar(x1[:, n, :], x1[:, n, :], stat_a[:, n, 6:7], rstd_a[:, n:n + 1],
                                              ALU.subtract, ALU.mult).then_inc(x1_ready, 1)
                    if name == "ht":
                        l, = arg
                        for u, w in enumerate((2, 1)):
                            hs = slice(2 * u, 2 * u + w)
                            if l == 0:
                                dve.wait_ge(h_hi_s, at(tb, 4, u + 1))
                                dve.tensor_tensor(h_lo[:, hs, :],
                                                  b_bank(l, f"T{u}")[:, 0:w * N].rearrange("p (c n) -> p c n", c=w),
                                                  r32(h_hi[:, hs, :]), ALU.subtract).then_inc(h_lo_s, 1)
                            else:
                                dve.wait_ge(h_f32, at(tb, HC, 2 * u + w))
                                if u == 0:
                                    dve.wait_ge(u_full, at(tb, 4, 2))
                                    dve.wait_ge(l_full, at(tb, 4, 2))
                                dve.tensor_copy(h_hi[:, hs, :], hT[:, hs, :]).then_inc(h_hi_s, 1)
                                dve.wait_ge(h_hi_s, at(tb, 4, 2 + u + 1))
                                dve.tensor_tensor(h_lo[:, hs, :], hT[:, hs, :], r32(h_hi[:, hs, :]),
                                                  ALU.subtract).then_inc(h_lo_s, 1)
                    if name == "m":
                        l, u = arg
                        dve.wait_ge(m_hi_s, at(tb, 6, 3 * l + u + 1))
                        dve.tensor_tensor(m_lo[:, 2 * u:2 * u + 2, :],
                                          b_bank(l, f"M{u}")[:, :].rearrange("p (c n) -> p c n", c=2),
                                          r32(m_hi[:, 2 * u:2 * u + 2, :]), ALU.subtract).then_inc(m_lo_s, 1)
                    if name == "lin":
                        l, = arg
                        for n in range(NT):
                            dve.wait_ge(l_hi_s, at(tb, 4, 2 * l + n + 1))
                            dve.tensor_tensor(l_lo[:, n, 0:H], b_bank(l, f"L{n}")[:, 0:H], r32(l_hi[:, n, 0:H]),
                                              ALU.subtract).then_inc(l_lo_s, 1)
                    if name == "u":
                        l, = arg
                        if l == 0:
                            dve.wait_ge(masks, at(tb, 1, 1))
                            if not first_b:
                                dve.wait_ge(u_exp, at(tb - 1, 4, 4))
                        else:
                            dve.wait_ge(h_lo_s, at(tb, 4, 4))
                        for J in range(NT):
                            dve.wait_ge(u_full, at(tb, 4, 2 * l + J + 1))
                            dve.tensor_tensor(um[:, J, :], b_bank(l, f"U{J}")[:, 0:3 * P], mask[:, J, :],
                                              ALU.mult).then_inc(u_mask, 1)
                        for J in range(NT):
                            dve.wait_ge(u_mask, at(tb, 4, 2 * l + J + 1))
                            o = 2 * J * P
                            dve.tensor_tensor(um[:, J, P:2 * P], um[:, J, P:2 * P], um[:, J, o:o + P],
                                              ALU.add).then_inc(u_add, 1)
                    if name == "e":
                        l, = arg
                        dve.wait_ge(e_hi_s, at(tb, 2, l + 1))
                        dve.tensor_tensor(e_lo, ex[:, :, :], r32(e_hi), ALU.subtract).then_inc(e_lo_s, 1)
                    if name == "ctx":
                        l, = arg
                        for n in range(NT):
                            dve.wait_ge(c_full, at(tb, 4, 2 * l + n + 1))
                            if n == 0 and (l > 0 or not first_b):
                                dve.wait_ge(c_copy, at(tb, 4, 2) if l > 0 else at(tb - 1, 4, 4))
                            dve.tensor_scalar(den[:, n:n + 1], b_bank(l, f"C{n}")[:, H:H + 1], SUM_EPS, None,
                                              ALU.add).then_inc(c_den, 1)
                            dve.wait_ge(c_den, at(tb, 4, 2 * l + n + 1))
                            dve.reciprocal(rden[:, n:n + 1], den[:, n:n + 1]).then_inc(c_rden, 1)
                    if name == "z":
                        normalise(tb, 0)
                    if name == "zc":
                        normalise(tc, 1)
                    if name == "residual":
                        dve.wait_ge(res_kept, at(tc, 1, 1))
                        for n in range(NT):
                            dve.wait_ge(f_add, at(tc, NT, n + 1))
                            dve.scalar_tensor_tensor(out=cz[:, n, :], in0=cz[:, n, :], scalar=0.0,
                                                     in1=x1_res[:, n, :], op0=ALU.max,
                                                     op1=ALU.add).then_inc(f_res, 1)
                        for n in range(NT):
                            dve.wait_ge(f_res, at(tc, NT, n + 1))
                            dve.bn_stats(stat_b[:, n, 0:6], cz[:, n, :]).then_inc(f_stat, 1)
                        wait_apart(dve, f_stat, at(tc, NT, NT))
                        for n in range(NT):
                            dve.bn_aggr(stat_b[:, n, 6:8], stat_b[:, n, 0:6]).then_inc(f_aggr, 1)
                        dve.wait_ge(f_aggr, at(tc, NT, NT))
                        dve.tensor_scalar(std_b[:, :], stat_b[:, :, 7], LN_EPS, None,
                                          ALU.add).then_inc(f_var, 1)
                    if name == "store":
                        dve.wait_ge(f_rstd, at(tc, 1, 1))
                        for n in range(NT):
                            dve.tensor_scalar(cz[:, n, :], cz[:, n, :], stat_b[:, n, 6:7], std_b[:, n:n + 1],
                                              ALU.subtract, ALU.mult).then_inc(f_out, 1)

            turns(dve, body)

        @block.gpsimd
        def _(pool):
            pool.memset(ident[:, :], 0.0).then_inc(s_id, 1)
            pool.wait_ge(s_id, 1)
            pool.affine_select(out=ident[:, :], in_=ident[:, :], compare_op=ALU.not_equal, fill=1.0, base=0,
                               pattern=[[-1, P]], channel_multiplier=1).then_inc(s_id, 1)
            pool.memset(power[:, 0, :], -0.5).then_inc(s_pow, 1)
            pool.memset(power[:, 1, :], 0.5).then_inc(s_pow, 1)
            pool.wait_ge(s_pow, 2)
            pool.memset(r32(v_hi[:, :, :, :]), 0.0).then_inc(s_zero, 1)
            pool.memset(r32(v_lo[:, :, :, :]), 0.0).then_inc(s_zero, 1)
            pool.memset(r32(l_hi[:, :, H:H + 2]), 1.0).then_inc(s_zero, 1)
            pool.memset(r32(l_lo[:, :, H:H + 2]), 0.0).then_inc(s_zero, 1)
            pool.wait_ge(s_col, 64)

            def body(ta, tb, tc, first_a, first_b, more):
                for name, arg in steps("pool", ta, tb, tc):
                    if name == "AT":
                        pool.wait_ge(at_done, at(ta, 1, 1))
                        if not first_a:
                            wait_apart(pool, u_mask, at(ta - 1, 4, 4))
                        for o, src, cm, st, base, w in (
                                (mask[:, 0, 0:P], adjT[:, 0, 0:P], 1, -1, 0, P),
                                (mask[:, 0, P:3 * P], adj_in[:, 0, :], -1, 1, -1, N),
                                (mask[:, 1, 0:2 * P], adjT[:, 1, :], 1, -1, P, N),
                                (mask[:, 1, 2 * P:3 * P], adj_in[:, 1, P:N], -1, 1, -1, P)):
                            ins = pool.affine_select(out=o, in_=src, compare_op=ALU.is_ge, fill=0.0, base=base,
                                                     pattern=[[st, w]], channel_multiplier=cm)
                        ins.then_inc(masks, 1)
                    if name == "O":
                        pool.wait_ge(a_var, at(ta, 1, 1))
                        pool.tensor_tensor(rstd_a[:, :], rstd_a[:, :], power[:, 0, :], ALU.pow).then_inc(a_rstd, 1)
                    if name in ("z", "zc"):
                        pool.wait_ge(b_var, at(tb, 2, 1) if name == "z" else at(tc, 2, 2))
                        pool.tensor_tensor(std_b[:, :], std_b[:, :], power[:, 1, :], ALU.pow).then_inc(b_std, 1)
                    if name == "keep":
                        pool.wait_ge(t_full, at(tb, 4, 2))
                        if not first_b:
                            wait_apart(pool, f_res, at(tb - 1, NT, NT))
                        pool.tensor_copy(x1_res[:, :, :], x1[:, :, :]).then_inc(res_kept, 1)
                    if name == "e":
                        l, = arg
                        pool.wait_ge(u_exp, at(tb, 4, 2 * l + 2))
                        pool.tensor_tensor(ex[:, :, :], ex[:, :, :], adjT[:, :, :], ALU.mult).then_inc(u_adj, 1)
                    if name == "affine":
                        for n in range(NT):
                            pool.wait_ge(z_ready, at(tc, 4, 2 + n + 1))
                            pool.tensor_tensor(cz[:, n, :], cz[:, n, :], a_row[:, :], ALU.mult).then_inc(f_mul, 1)
                            pool.wait_ge(f_mul, at(tc, NT, n + 1))
                            pool.tensor_tensor(cz[:, n, :], cz[:, n, :], b_row[:, :], ALU.add).then_inc(f_add, 1)
                    if name == "residual":
                        pool.wait_ge(f_var, at(tc, 1, 1))
                        pool.tensor_tensor(std_b[:, :], std_b[:, :], power[:, 0, :], ALU.pow).then_inc(f_rstd, 1)

            turns(pool, body)


_INS = ["x", "adj", "L0_gnn_Wq", "L0_gnn_Wk", "L0_gnn_Wv", "L0_gnn_bv", "L0_gnn_Wo", "L0_gnn_bo",
        "L1_gnn_W_left", "L1_gnn_W_right", "L1_gnn_W_lin", "L1_gnn_b_lin", "L1_gnn_ln_a", "L1_gnn_ln_b"]
_OUTS = [((32, 256, 384), "float32")]


def kernel(**inputs):
    import numpy as _np
    import concourse.bacc as _bacc
    from concourse import mybir as _mybir
    from concourse.bass_utils import run_bass_kernel_spmd as _run

    nc = _bacc.Bacc("TRN2", target_bir_lowering=False, num_devices=1)
    arrays, args = {}, []
    for name in _INS:
        a = _np.ascontiguousarray(inputs[name])
        arrays[f"in_{name}_dram"] = a
        args.append(nc.dram_tensor(f"in_{name}_dram", a.shape, _mybir.dt.from_np(a.dtype), kind="ExternalInput").ap())
    for i, (shape, dtype) in enumerate(_OUTS):
        dt = _mybir.dt.from_np(_np.dtype(dtype))
        args.append(nc.dram_tensor(f"out_{i}_dram", shape, dt, kind="ExternalOutput").ap())
    adj_resnorm_kernel(nc, *args)
    r = _run(nc, [arrays], core_ids=[0])
    got = tuple(r.results[0][f"out_{i}_dram"] for i in range(len(_OUTS)))
    return got[0]
```

```python
from contextlib import ExitStack

import concourse.bass as bass
from concourse import mybir

P = 128
F32 = mybir.dt.float32
F32R = mybir.dt.float32r
ALU = mybir.AluOpType
ACT = mybir.ActivationFunctionType

LN_EPS = 1e-5
STD_EPS = 1e-3
SUM_EPS = 1e-10


def at(turn, per_turn, k):
    return turn * per_turn + k


def adj_resnorm_kernel(nc, x, adj, Wq, Wk, Wv, bv, Wo, bo, Wl, Wr, Wlin, b_lin, ln_a, ln_b, out):
    B, N, H = x.shape
    LAYERS = Wl.shape[0]
    HEADS = 12
    HD = H // HEADS
    NT = N // P
    HC = H // P
    PER = P // HD
    PAIRS = HEADS // 2
    SCALE = float(H) ** -0.5
    assert (NT, HC, PER, LAYERS) == (2, 3, 4, 2)

    MATS = [Wq, Wk, Wv, Wo] + [w[l] for l in range(LAYERS) for w in (Wl, Wr, Wlin)]
    Q_, K_, V_, O_ = range(4)
    LEFT, RIGHT, LIN = (lambda l: 4 + 3 * l), (lambda l: 5 + 3 * l), (lambda l: 6 + 3 * l)
    BIAS = [bv, bo] + [b_lin[l] for l in range(LAYERS)]
    BV, BO, BL = 0, 1, 2
    VAL = [0, 128, 224, 352]
    SLOT = [VAL[j] - HD * j for j in range(PER)]
    VW = VAL[-1] + HD
    SLICES = len(MATS) * HC
    EARLY = LEFT(0) * HC
    NSTAGE = 5
    LSTAGE = 6

    with ExitStack() as ctx:
        def sb(name, shape, dt=F32):
            return ctx.enter_context(nc.sbuf_tensor(name, shape, dt))

        def sem(name):
            return ctx.enter_context(nc.semaphore(name))

        w_hi = sb("w_hi", [P, len(MATS), HC, H], F32R)
        w_lo = sb("w_lo", [P, len(MATS), HC, H], F32R)
        ident = sb("ident", [P, P])
        power = sb("power", [P, 2, NT])
        a_col = sb("a_col", [P, HC])
        b_col = sb("b_col", [P, HC])
        a_row = sb("a_row", [P, H])
        b_row = sb("b_row", [P, H])
        xin = sb("xin", [P, NT, H])
        adj_in = sb("adj_in", [P, NT, N])
        xo_hi = sb("xo_hi", [P, HC, N], F32R)
        xo_lo = sb("xo_lo", [P, HC, N], F32R)
        qk_part = sb("qk_part", [P, 2, 4, N], F32R)
        pt_hi = qk_part[:, 0, :, :]
        pt_lo = qk_part[:, 1, :, :]
        stack = sb("stack", [P, 2, HEADS, N], F32R)
        SR = 3 * HD
        v_hi = sb("v_hi", [P, NT, HC, VW], F32R)
        v_lo = sb("v_lo", [P, NT, HC, VW], F32R)
        prob = sb("prob", [P, 2, 2, NT, N])
        junk = sb("junk", [P, NT, N], mybir.dt.bfloat16)
        nmax = sb("nmax", [P, HEADS, NT])
        asum = sb("asum", [P, HEADS, NT])
        esum = sb("esum", [P, HEADS, NT])
        rsum = sb("rsum", [P, HEADS, NT])
        x1 = sb("x1", [P, NT, H])
        stat_a = sb("stat_a", [P, NT, 8])
        rstd_a = sb("rstd_a", [P, NT])
        x1_res = sb("x1_res", [P, NT, H])
        adjT = sb("adjT", [P, NT, N])
        mask = sb("mask", [P, NT, 3 * P])
        h_hi = sb("h_hi", [P, HC, N], F32R)
        h_lo = sb("h_lo", [P, HC, N], F32R)
        m_hi = sb("m_hi", [P, 2 * HC, N], F32R)
        m_lo = sb("m_lo", [P, 2 * HC, N], F32R)
        l_hi = sb("l_hi", [P, NT, H + 2], F32R)
        l_lo = sb("l_lo", [P, NT, H + 2], F32R)
        um = sb("um", [P, NT, 3 * P])
        hT = um[:, :, :].rearrange("p a b -> p (a b)").rearrange("p (c n) -> p c n", c=HC)
        ex = sb("ex", [P, NT, N])
        e_hi = m_hi[:, 0:NT, :]
        e_lo = m_lo[:, 0:NT, :]
        cz = sb("cz", [P, NT, H])
        stat_b = sb("stat_b", [P, NT, 8])
        den = sb("den", [P, NT])
        std_b = sb("std_b", [P, NT])
        sden = sb("sden", [P, NT])
        zfac = sb("zfac", [P, NT])
        zoff = sb("zoff", [P, NT])
        stat_f = sb("stat_f", [P, NT, 8])
        rstd_f = sb("rstd_f", [P, NT])
        def r32(ap):
            return ap.bitcast(F32)

        def bias_at(first, second, n):
            return (first, second)[n // 2][0:1].rearrange("p a b -> p (a b)")[:, n % 2 * H:(n % 2 + 1) * H]

        bias_raw = [bias_at(cz[:, :, :], um[:, :, :], n) for n in range(len(BIAS))]
        bias_hi, bias_lo = ([m[0:1, :, :].rearrange("p a b -> p (a b)")[:, n * H:(n + 1) * H]
                             for n in range(len(BIAS))] for m in (m_hi, m_lo))
        wstage = prob[:, :, :, :, :].rearrange("p a b c d -> p (a b c d)")
        lstage = [m[:, :, :].rearrange("p a b -> p (a b)") for m in (x1_res, cz, um)]

        def w_slice(i):
            if i < EARLY:
                return wstage[:, i % NSTAGE * H:(i % NSTAGE + 1) * H], s_w[i % NSTAGE], 16 * (i // NSTAGE + 1)
            k, turn = (i - EARLY) % LSTAGE, (i - EARLY) // LSTAGE
            return lstage[k // 2][:, k % 2 * H:(k % 2 + 1) * H], s_w[NSTAGE + k], 16 * (turn + 1)

        def w_bank(i):
            return bank[i % 4 if i < EARLY else 5 + (i - EARLY) % 3]


        bank = [ctx.enter_context(nc.psum_tensor(f"bank{i}", [P, 512], F32)) for i in range(8)]
        ov_bank = bank[4]
        s_w = [sem(f"weight_landed{i}") for i in range(NSTAGE + LSTAGE)]
        s_wt = sem("weight_turned")
        s_whi = sem("weight_hi")
        s_wlo = sem("weight_lo")
        s_id = sem("identity_made")
        s_bias = sem("bias_landed")
        s_bhi = sem("bias_hi")
        s_blo = sem("bias_lo")
        s_brow = sem("bias_rows_placed")
        s_col = sem("ln_vectors_landed")
        s_zero = sem("padding_made")
        s_pow = sem("exponents_made")
        passed = {nc.vector.engine: sem("vector_wait_passed"), nc.gpsimd.engine: sem("gpsimd_wait_passed")}
        x_in = sem("x_landed")
        adj_ld = sem("adj_landed")
        x_res = sem("x_residual_landed")
        xt_full = sem("xt_in_psum")
        xt_hi = sem("xt_hi_done")
        xt_lo = sem("xt_lo_done")
        qk_full = sem("qk_in_psum")
        qk_hi = sem("qk_hi_done")
        qk_lo = sem("qk_lo_done")
        stacked = [sem(f"stacked{g}") for g in range(PAIRS)]
        v_full = sem("v_in_psum")
        v_hi_s = sem("v_hi_done")
        v_lo_s = sem("v_lo_done")
        s_full = sem("scores_in_psum")
        s_neg = sem("scores_negated")
        s_abs = sem("scores_abs_summed")
        s_exp = sem("exp_done")
        s_rec = sem("esum_inverted")
        s_rn = sem("row_factor_ready")
        s_norm = sem("probs_normalised")
        pt_full = sem("pt_in_psum")
        pt_hi_s = sem("pt_hi_done")
        pt_lo_s = sem("pt_lo_done")
        pv_used = sem("pv_products_done")
        ot_hi = sem("heads_out_hi_done")
        ot_lo = sem("heads_out_lo_done")
        o_full = sem("o_in_psum")
        o_sum = sem("residual_added")
        a_stat = sem("x1_stats")
        a_aggr = sem("x1_stats_joined")
        a_var = sem("x1_var_ready")
        a_rstd = sem("x1_rstd")
        x1_ready = sem("x1_ready")
        at_full = sem("adjt_in_psum")
        at_done = sem("adjt_copied")
        masks = sem("masks_made")
        res_kept = sem("x1_residual_kept")
        t_full = sem("ht_in_psum")
        h_f32 = sem("ht_relu_done")
        h_hi_s = sem("h_hi_done")
        h_lo_s = sem("h_lo_done")
        m_full = sem("m_in_psum")
        m_hi_s = sem("m_hi_done")
        m_lo_s = sem("m_lo_done")
        l_full = sem("hlin_in_psum")
        l_hi_s = sem("hlin_hi_done")
        l_lo_s = sem("hlin_lo_done")
        u_full = sem("u_in_psum")
        u_mask = sem("u_masked")
        u_add = sem("u_halves_added")
        u_exp = sem("u_exp_done")
        u_adj = sem("u_exp_times_adj")
        e_hi_s = sem("e_hi_done")
        e_lo_s = sem("e_lo_done")
        c_full = sem("ctx_in_psum")
        c_den = sem("ctx_den_ready")
        b_stat = sem("ctx_stats")
        b_aggr = sem("ctx_stats_joined")
        b_std = sem("ctx_std")
        b_stde = sem("ctx_std_plus_eps")
        b_fac = sem("ctx_factor")
        b_off = sem("ctx_offset")
        z_ready = sem("ctx_normalised")
        f_mul = sem("final_scaled")
        f_add = sem("final_shifted")
        f_res = sem("final_residual_added")
        f_stat = sem("final_stats")
        f_aggr = sem("final_stats_joined")
        f_var = sem("final_var_ready")
        f_rstd = sem("final_rstd")
        f_out = sem("final_ready")
        stored = sem("out_stored")

        A_STEPS = {"XT", "QK", "V", "S", "N", "T", "PV", "AT", "O", "LN"}
        B_STEPS = {"keep", "ht", "m", "lin", "u", "e", "ctx", "z"}
        C_STEPS = {"zc", "affine", "residual", "store"}
        ORDERS = {
            "sp": [
                ("XT",), ("QK", 0), ("QK", 1), ("QK", 2), ("store",), ("V",), ("AT",),
            ],
            "pe": [
                ("XT",), ("QK", 0), ("QK", 1), ("ht", 0), ("m", 0, 0), ("QK", 2), ("S", 0), ("m", 0, 1),
                ("m", 0, 2), ("S", 1), ("V",), ("u", 0), ("S", 2), ("lin", 0), ("T", 0), ("ctx", 0), ("S", 3),
                ("PV", 0), ("T", 1), ("ht", 1), ("PV", 1), ("T", 2), ("S", 4), ("m", 1, 0), ("S", 5),
                ("lin", 1), ("PV", 2), ("T", 3), ("m", 1, 1), ("m", 1, 2), ("PV", 3), ("T", 4), ("u", 1),
                ("PV", 4), ("T", 5), ("PV", 5), ("O",), ("ctx", 1), ("AT",),
            ],
            "act": [
                ("XT",), ("QK", 0), ("zc",), ("ht", 0), ("QK", 1), ("m", 0, 0), ("m", 0, 1), ("QK", 2),
                ("m", 0, 2), ("S", 0), ("V",), ("S", 1), ("u", 0), ("e", 0), ("lin", 0), ("T", 0), ("S", 2),
                ("z", 0), ("T", 1), ("ht", 1), ("S", 3), ("PV", 1), ("T", 2), ("m", 1, 0), ("lin", 1), ("S", 4),
                ("T", 3), ("m", 1, 1), ("m", 1, 2), ("S", 5), ("PV", 3), ("T", 4), ("T", 5), ("u", 1),
                ("PV", 5), ("e", 1), ("AT",),
            ],
            "dve": [
                ("XT",), ("zc",), ("QK", 0), ("ht", 0), ("QK", 1), ("m", 0, 0), ("residual",), ("S", 0),
                ("m", 0, 1), ("store",), ("m", 0, 2), ("QK", 2), ("S", 1), ("V",), ("N", 0), ("u", 0), ("N", 1),
                ("e", 0), ("lin", 0), ("S", 2), ("ctx", 0), ("T", 0), ("z", 0), ("N", 2), ("T", 1), ("S", 3),
                ("ht", 1), ("S", 4), ("PV", 1), ("T", 2), ("N", 3), ("m", 1, 0), ("lin", 1), ("S", 5), ("T", 3),
                ("m", 1, 1), ("N", 4), ("m", 1, 2), ("PV", 3), ("T", 4), ("N", 5), ("u", 1), ("T", 5),
                ("PV", 5), ("e", 1), ("O",), ("ctx", 1), ("LN",),
            ],
            "pool": [
                ("affine",), ("residual",), ("keep",), ("e", 0), ("ctx", 0), ("e", 1), ("O",), ("ctx", 1),
                ("AT",),
            ],
        }

        HELD = {"ht": ("T0", "T1"), "lin": ("L0", "L1"), "u": ("U0", "U1"), "ctx": ("C0", "C1")}
        UNITS = [(l[0], u) for name, *l in ORDERS["pe"] if name in B_STEPS
                 for u in ([f"M{l[1]}"] if name == "m" else HELD.get(name, ()))]
        LAST = {"T0": (h_lo_s, 4, 1), "T1": (h_lo_s, 4, 2), "M0": (m_lo_s, 6, 1), "M1": (m_lo_s, 6, 2),
                "M2": (m_lo_s, 6, 3), "L0": (l_lo_s, 4, 1), "L1": (l_lo_s, 4, 2), "U0": (u_mask, 4, 1),
                "U1": (u_mask, 4, 2), "C0": (z_ready, 4, 1), "C1": (z_ready, 4, 2)}

        LATE_AFTER = {"pool": {}, "sp": {"QK": 2, "V": 6}}
        for eng in ("pe", "act", "dve"):
            LATE_AFTER[eng] = {"QK": 2, "S": 1, "T": 2}

        def b_bank(l, u):
            return bank[5 + UNITS.index((l, u)) % 3]

        def b_bank_free(pe, l, u, tb, first):
            i = UNITS.index((l, u))
            before = [k for k in range(len(UNITS)) if k % 3 == i % 3]
            n = before.index(i)
            pl, pu = UNITS[before[n - 1]]
            s, per, k = LAST[pu]
            if n > 0:
                pe.wait_ge(s, at(tb, per, pl * per // LAYERS + k))
            elif not first:
                pe.wait_ge(s, at(tb - 1, per, pl * per // LAYERS + k))

        def v_view(v, n, a):
            o = VAL[2 * a]
            return v[:, n, :, o:o + 160].rearrange("p c (j w) -> p c j w", w=32)[:, :, 0:5:4, :]

        def v_src(n, a):
            return bank[2 + n][:, 0:H].rearrange("p (c j w) -> p c j w", c=HC, w=HD)[:, :, 2 * a:2 * a + 2, :]

        def steps(eng, ta, tb, tc):
            late = EARLY
            for name, *arg in ORDERS[eng]:
                t = ta if name in A_STEPS else tb if name in B_STEPS else tc
                if t is not None:
                    yield name, arg
                    for _ in range(LATE_AFTER[eng].get(name, 0) if ta is not None and tb is None else 0):
                        if late < SLICES:
                            yield "W", [late]
                            late += 1

        def turns(eng, body):
            body(0, None, None, True, True, True)
            body(1, 0, None, False, True, True)
            with eng.Fori(2, B - 1) as t:
                body(t, t - 1, t - 2, False, False, True)
            body(B - 1, B - 2, B - 3, False, False, False)
            body(None, B - 1, B - 2, False, False, False)
            body(None, None, B - 1, False, False, False)

        def wait_apart(eng, s, value):
            eng.wait_ge(s, value)
            eng.sem_inc(passed[eng.engine], 1)

        block = ctx.enter_context(nc.Block())

        @block.sync
        def _(sp):
            def load_x(t):
                sp.dma_start(xin[:, :, :], x[t, :, :].rearrange("(n p) h -> p n h", p=P)).then_inc(x_in, 16)

            def load_adj(t):
                sp.dma_start(adj_in[:, :, :], adj[t, :, :].rearrange("(n p) m -> p n m", p=P)).then_inc(adj_ld, 16)

            def load_slice(i):
                to, landed, _ = w_slice(i)
                sp.dma_start(to, MATS[i // HC][i % HC * P:(i % HC + 1) * P, :]).then_inc(landed, 16)

            for i in range(EARLY):
                if i >= NSTAGE:
                    sp.wait_ge(s_wt, i - NSTAGE + 1)
                load_slice(i)
                if i == 7:
                    load_x(0)
                    load_adj(0)
                if i == NSTAGE - 1:
                    for n, b in enumerate(BIAS):
                        sp.dma_start(bias_raw[n], b.rearrange("(a h) -> a h", a=1)).then_inc(s_bias, 16)
                    sp.dma_start(a_col[:, :], ln_a[0, :].rearrange("(c p) -> p c", p=P),
                                 allow_slow_non_contiguous=True).then_inc(s_col, 16)
                    sp.dma_start(b_col[:, :], ln_b[0, :].rearrange("(c p) -> p c", p=P),
                                 allow_slow_non_contiguous=True).then_inc(s_col, 16)
                    sp.dma_start(a_row[:, :], ln_a[1, :].partition_broadcast(P)).then_inc(s_col, 16)
                    sp.dma_start(b_row[:, :], ln_b[1, :].partition_broadcast(P)).then_inc(s_col, 16)
            sp.wait_ge(s_blo, len(BIAS))
            for n in range(len(BIAS)):
                for part, row in ((bias_hi, SR), (bias_lo, SR + 1)):
                    sp.dma_start(r32(stack[row:row + 1, 0, 2 * n:2 * n + 2, :].rearrange("p a b -> p (a b)")[:, 0:H]),
                                 r32(part[n])).then_inc(s_brow, 16)
            for i in range(EARLY, EARLY + LSTAGE):
                load_slice(i)

            def body(ta, tb, tc, first_a, first_b, more):
                for name, arg in steps("sp", ta, tb, tc):
                    if name == "XT" and more:
                        sp.wait_ge(xt_full, at(ta, 2, 2))
                        load_x(ta + 1)
                    if name == "W" and arg[0] + LSTAGE < SLICES:
                        sp.wait_ge(s_wt, arg[0] + 1)
                        load_slice(arg[0] + LSTAGE)
                    if name == "QK":
                        c, = arg
                        sp.wait_ge(qk_lo, at(ta, HC, c + 1))
                        part = qk_part[:, c % 2, :, :]
                        for j in range(PER):
                            src = part[HD * j:HD * (j + 1), :, :]
                            h = PER * c + j
                            for r, (a, step) in enumerate(((0, 2), (0, 3), (1, 1))):
                                sp.dma_start(r32(stack[HD * r:HD * (r + 1), :, h, :]),
                                             r32(src[:, a:a + step + 1:step, :])).then_inc(stacked[h // 2], 16)
                    if name == "V":
                        if not first_a:
                            sp.wait_ge(res_kept, at(ta - 1, 1, 1))
                        sp.dma_start(x1[:, :, :], x[ta, :, :].rearrange("(n p) h -> p n h", p=P)).then_inc(x_res, 16)
                    if name == "AT" and more:
                        sp.wait_ge(masks, at(ta, 1, 1))
                        load_adj(ta + 1)
                    if name == "store":
                        sp.wait_ge(f_out, at(tc, 2, 2))
                        sp.dma_start(out[tc, :, :].rearrange("(n p) h -> p n h", p=P), cz[:, :, :]).then_inc(stored, 16)

            turns(sp, body)
            sp.wait_ge(stored, 16 * B)

        @block.tensor
        def _(pe):
            def mm3(o, lh, ll, rh, rl, start, stop):
                pe.matmul(o, lh, rh, start=start, stop=False)
                pe.matmul(o, lh, rl, start=False, stop=False)
                return pe.matmul(o, ll, rh, start=False, stop=stop)

            def moving_late(o, terms, hi, lo):
                for k, (lh, ll, rh, rl) in enumerate(terms):
                    if hi[k]:
                        pe.wait_ge(*hi[k])
                    pe.matmul(o, lh, rh, start=k == 0, stop=False)
                    pe.matmul(o, ll, rh, start=False, stop=False)
                for k, (lh, ll, rh, rl) in enumerate(terms):
                    if lo[k]:
                        pe.wait_ge(*lo[k])
                    mm = pe.matmul(o, lh, rl, start=False, stop=k == len(terms) - 1)
                return mm

            def bias(o, n, start):
                return pe.matmul(o, stack[SR:SR + 2, 1, 0, 0:P],
                                 stack[SR:SR + 2, 0, 2 * n:2 * n + 2, :].rearrange("p a b -> p (a b)")[:, 0:H],
                                 start=start, stop=False)

            pe.wait_ge(s_id, 2)

            def turn_slice(i):
                src, landed, count = w_slice(i)
                pe.wait_ge(landed, count)
                if EARLY > i >= 4:
                    pe.wait_ge(s_wlo, i - 3)
                elif i >= EARLY + 3:
                    pe.wait_ge(s_wlo, i - 2)
                for c in range(HC):
                    mm = pe.transpose(w_bank(i)[:, c * P:(c + 1) * P], src[:, c * P:(c + 1) * P], ident[:, :])
                mm.then_inc(s_wt, 1)

            for i in range(EARLY):
                turn_slice(i)
            pe.wait_ge(s_wlo, EARLY)

            def body(ta, tb, tc, first_a, first_b, more):
                if first_b and tb is not None:
                    pe.wait_ge(s_wlo, SLICES)
                for name, arg in steps("pe", ta, tb, tc):
                    if name == "W":
                        turn_slice(arg[0])
                    if name == "XT":
                        pe.wait_ge(x_in, at(ta, 16, 16))
                        for u, cs in enumerate(((0, 1), (2,))):
                            if not first_a:
                                pe.wait_ge(o_sum, at(ta - 1, 2, u + 1))
                            for c in cs:
                                for n in range(NT):
                                    mm = pe.transpose(bank[u][:, (c % 2) * N + n * P:(c % 2) * N + (n + 1) * P],
                                                      xin[:, n, c * P:(c + 1) * P], ident[:, :])
                            mm.then_inc(xt_full, 1)
                    if name == "QK":
                        m, = arg
                        if m == 0:
                            if not first_a:
                                pe.wait_ge(at_done, at(ta - 1, 1, 1))
                            first_hi = ((xt_hi, at(ta, 2, 1)), None, (xt_hi, at(ta, 2, 2)))
                            first_lo = ((xt_lo, at(ta, 2, 1)), None, (xt_lo, at(ta, 2, 2)))
                        if m == 1 and not first_a:
                            pe.wait_ge(pt_lo_s, at(ta - 1, HEADS, HEADS))
                        if m == 2 and not first_a:
                            pe.wait_ge(ot_lo, at(ta - 1, HC, HC))
                        b = bank[2 + m]
                        for half, w in enumerate((Q_, K_)):
                            fresh = m == 0 and half == 0
                            ms = slice(m * P, (m + 1) * P)
                            mm = moving_late(b[:, half * N:(half + 1) * N],
                                             [(w_hi[:, w, c, ms], w_lo[:, w, c, ms], xo_hi[:, c, :], xo_lo[:, c, :])
                                              for c in range(HC)],
                                             first_hi if fresh else 3 * [None], first_lo if fresh else 3 * [None])
                        mm.then_inc(qk_full, 1)
                    if name == "V":
                        if first_a:
                            pe.wait_ge(s_brow, 16 * 2 * len(BIAS))
                            pe.wait_ge(s_zero, 5)
                        for n in range(NT):
                            pe.wait_ge(qk_lo, at(ta, HC, n + 1))
                            o = bank[2 + n][:, 0:H]
                            bias(o, BV, True)
                            for c in range(HC):
                                mm = mm3(o, xo_hi[:, c, n * P:(n + 1) * P], xo_lo[:, c, n * P:(n + 1) * P],
                                         w_hi[:, V_, c, :], w_lo[:, V_, c, :], False, c == HC - 1)
                            mm.then_inc(v_full, 1)
                    if name == "S":
                        for h in (2 * arg[0], 2 * arg[0] + 1):
                            if h % 2 == 0:
                                pe.wait_ge(stacked[h // 2], at(ta, 16 * 6, 16 * 6))
                            if h >= 2:
                                pe.wait_ge(s_neg, at(ta, 2 * HEADS, 2 * (h - 1)))
                            for n in range(NT):
                                mm = pe.matmul(bank[h % 2][:, n * N:(n + 1) * N],
                                               stack[0:SR, 0, h, n * P:(n + 1) * P], stack[0:SR, 1, h, :],
                                               start=True, stop=True)
                            mm.then_inc(s_full, 1)
                    if name == "T":
                        g, = arg
                        for i in range(2):
                            h = 2 * g + i
                            pe.wait_ge(s_norm, at(ta, HEADS, h + 1))
                            if g == 0:
                                pe.wait_ge(v_lo_s, at(ta, 2 * NT, 2 * i + 2))
                            else:
                                pe.wait_ge(pt_lo_s, at(ta, HEADS, h - 1))
                            for kt in range(NT):
                                for n in range(NT):
                                    mm = pe.transpose(bank[2 + i][:, kt * N + n * P:kt * N + (n + 1) * P],
                                                      prob[:, g % 2, i, n, kt * P:(kt + 1) * P], ident[:, :])
                            mm.then_inc(pt_full, 1)
                    if name == "PV":
                        g, = arg
                        c = g // 2
                        if g % 2 == 0:
                            if c > 0:
                                pe.wait_ge(ot_lo, at(ta, HC, c))
                            else:
                                pe.wait_ge(qk_lo, at(ta, HC, HC))
                        for i in range(2):
                            j = 2 * (g % 2) + i
                            sl = slice(SLOT[j], SLOT[j] + P)
                            pe.wait_ge(pt_hi_s, at(ta, HEADS, 2 * g + i + 1))
                            for kt in range(NT):
                                rh = pt_hi[:, 2 * i + kt, :]
                                pe.matmul(ov_bank[:, 0:N], v_hi[:, kt, c, sl], rh, start=j == 0 and kt == 0, stop=False)
                                pe.matmul(ov_bank[:, 0:N], v_lo[:, kt, c, sl], rh, start=False, stop=False)
                            pe.wait_ge(pt_lo_s, at(ta, HEADS, 2 * g + i + 1))
                            for kt in range(NT):
                                mm = pe.matmul(ov_bank[:, 0:N], v_hi[:, kt, c, sl], pt_lo[:, 2 * i + kt, :],
                                               start=False, stop=j == PER - 1 and kt == NT - 1)
                        mm.then_inc(pv_used, 1)
                    if name == "AT":
                        pe.wait_ge(pt_lo_s, at(ta, HEADS, HEADS - 1))
                        for J in range(NT):
                            for n in range(NT):
                                mm = pe.transpose(bank[2][:, J * N + n * P:J * N + (n + 1) * P],
                                                  adj_in[:, n, J * P:(J + 1) * P], ident[:, :])
                        mm.then_inc(at_full, 1)
                    if name == "O":
                        pe.wait_ge(s_neg, at(ta, 2 * HEADS, 2 * HEADS))
                        pe.wait_ge(ot_lo, at(ta, HC, HC - 1))
                        for n in range(NT):
                            o = bank[n][:, 0:H]
                            ns = slice(n * P, (n + 1) * P)
                            bias(o, BO, True)
                            for c in range(HC - 1):
                                mm3(o, xo_hi[:, c, ns], xo_lo[:, c, ns], w_hi[:, O_, c, :], w_lo[:, O_, c, :],
                                    False, False)
                            c = HC - 1
                            pe.wait_ge(ot_hi, at(ta, HC, HC))
                            pe.matmul(o, xo_hi[:, c, ns], w_hi[:, O_, c, :], start=False, stop=False)
                            pe.matmul(o, xo_hi[:, c, ns], w_lo[:, O_, c, :], start=False, stop=False)
                            pe.wait_ge(ot_lo, at(ta, HC, HC))
                            mm = pe.matmul(o, xo_lo[:, c, ns], w_hi[:, O_, c, :], start=False, stop=True)
                            mm.then_inc(o_full, 1)
                    if name == "ht":
                        l, = arg
                        src = x1 if l == 0 else cz
                        for u, cs in enumerate(((0, 1), (2,))):
                            b_bank_free(pe, l, f"T{u}", tb, first_b)
                            b = b_bank(l, f"T{u}")
                            for n in range(NT):
                                if u == 0:
                                    ready = (x1_ready, at(tb, NT, n + 1)) if l == 0 else (z_ready, at(tb, 4, n + 1))
                                    pe.wait_ge(*ready)
                                for c in cs:
                                    mm = pe.transpose(b[:, (c % 2) * N + n * P:(c % 2) * N + (n + 1) * P],
                                                      src[:, n, c * P:(c + 1) * P], ident[:, :])
                            mm.then_inc(t_full, 1)
                    if name == "m":
                        l, u = arg
                        b_bank_free(pe, l, f"M{u}", tb, first_b)
                        if u == 0:
                            first_hi = ((h_hi_s, at(tb, 4, 2 * l + 1)), None, (h_hi_s, at(tb, 4, 2 * l + 2)))
                            first_lo = ((h_lo_s, at(tb, 4, 2 * l + 1)), None, (h_lo_s, at(tb, 4, 2 * l + 2)))
                        b = b_bank(l, f"M{u}")
                        for half in range(2):
                            k = 2 * u + half
                            w, m = (LEFT(l), k) if k < HC else (RIGHT(l), k - HC)
                            fresh = u == 0 and half == 0
                            ms = slice(m * P, (m + 1) * P)
                            mm = moving_late(b[:, half * N:(half + 1) * N],
                                             [(w_hi[:, w, c, ms], w_lo[:, w, c, ms], h_hi[:, c, :], h_lo[:, c, :])
                                              for c in range(HC)],
                                             first_hi if fresh else 3 * [None], first_lo if fresh else 3 * [None])
                        mm.then_inc(m_full, 1)
                    if name == "lin":
                        l, = arg
                        pe.wait_ge(h_lo_s, at(tb, 4, 2 * l + 2))
                        for n in range(NT):
                            b_bank_free(pe, l, f"L{n}", tb, first_b)
                            o = b_bank(l, f"L{n}")[:, 0:H]
                            bias(o, BL + l, True)
                            for c in range(HC):
                                mm = mm3(o, h_hi[:, c, n * P:(n + 1) * P], h_lo[:, c, n * P:(n + 1) * P],
                                         w_hi[:, LIN(l), c, :], w_lo[:, LIN(l), c, :], False, c == HC - 1)
                            mm.then_inc(l_full, 1)
                    if name == "u":
                        l, = arg
                        pe.wait_ge(m_lo_s, at(tb, 6, 3 * l + 2))
                        for J in range(NT):
                            b_bank_free(pe, l, f"U{J}", tb, first_b)
                            b = b_bank(l, f"U{J}")
                            js = slice(J * P, (J + 1) * P)
                            for side, lo, hi, to in ((0, 0, (J + 1) * P, 0), (1, J * P, N, (J + 1) * P)):
                                if side == 1 and J == 0:
                                    pe.wait_ge(m_lo_s, at(tb, 6, 3 * l + 3))
                                for c in range(HC):
                                    mm = mm3(b[:, to:to + hi - lo], m_hi[:, side * HC + c, js],
                                             m_lo[:, side * HC + c, js], h_hi[:, c, lo:hi], h_lo[:, c, lo:hi],
                                             c == 0, c == HC - 1)
                            mm.then_inc(u_full, 1)
                    if name == "ctx":
                        l, = arg
                        pe.wait_ge(l_lo_s, at(tb, 4, 2 * l + 2))
                        for n in range(NT):
                            b_bank_free(pe, l, f"C{n}", tb, first_b)
                            b = b_bank(l, f"C{n}")
                            for J in range(NT):
                                ns = slice(n * P, (n + 1) * P)
                                if n == 0:
                                    pe.wait_ge(e_hi_s, at(tb, 4, 2 * l + J + 1))
                                pe.matmul(b[:, 0:H + 2], e_hi[:, J, ns], l_hi[:, J, :], start=J == 0, stop=False)
                                pe.matmul(b[:, 0:H + 2], e_hi[:, J, ns], l_lo[:, J, :], start=False, stop=False)
                                if n == 0:
                                    pe.wait_ge(e_lo_s, at(tb, 4, 2 * l + J + 1))
                                mm = pe.matmul(b[:, 0:H + 2], e_lo[:, J, ns], l_hi[:, J, :], start=False,
                                               stop=J == NT - 1)
                            mm.then_inc(c_full, 1)

            turns(pe, body)

        @block.scalar
        def _(act):
            def slice_hi(i):
                act.wait_ge(s_wt, i + 1)
                act.activation(w_hi[:, i // HC, :, i % HC * P:(i % HC + 1) * P],
                               w_bank(i)[:, 0:H].rearrange("p (c o) -> p c o", c=HC), ACT.Copy,
                               scale=0.5 * SCALE if i // HC == Q_ else 1.0).then_inc(s_whi, 1)

            for i in range(EARLY):
                slice_hi(i)

            def body(ta, tb, tc, first_a, first_b, more):
                for name, arg in steps("act", ta, tb, tc):
                    if name == "W":
                        slice_hi(arg[0])
                    if name == "XT":
                        if not first_a:
                            act.wait_ge(o_full, at(ta - 1, NT, NT))
                        for u, w in enumerate((2, 1)):
                            act.wait_ge(xt_full, at(ta, 2, u + 1))
                            act.activation(xo_hi[:, 2 * u:2 * u + w, :],
                                           bank[u][:, 0:w * N].rearrange("p (c n) -> p c n", c=w),
                                           ACT.Copy).then_inc(xt_hi, 1)
                    if name == "QK":
                        m, = arg
                        act.wait_ge(qk_full, at(ta, HC, m + 1))
                        if m == 0 and not first_a:
                            act.wait_ge(pv_used, at(ta - 1, PAIRS, PAIRS))
                        if m == 2:
                            act.wait_ge(stacked[0], at(ta, 16 * 6, 16 * 6))
                            act.wait_ge(stacked[1], at(ta, 16 * 6, 16 * 6))
                        act.activation(qk_part[:, m % 2, 0:3:2, :],
                                       bank[2 + m][:, :].rearrange("p (a n) -> p a n", a=2),
                                       ACT.Copy).then_inc(qk_hi, 1)
                    if name == "V":
                        if not first_a:
                            act.wait_ge(pv_used, at(ta - 1, PAIRS, PAIRS))
                        for n in range(NT):
                            act.wait_ge(v_full, at(ta, NT, n + 1))
                            for a in range(2):
                                act.activation(v_view(v_hi, n, a), v_src(n, a), ACT.Copy).then_inc(v_hi_s, 1)
                    if name == "S":
                        g, = arg
                        for h in (2 * g, 2 * g + 1):
                            for n in range(NT):
                                k = 2 * h + n
                                act.wait_ge(s_neg, at(ta, 2 * HEADS, k + 1))
                                if k >= 2:
                                    act.wait_ge(s_abs, at(ta, 2 * HEADS, k - 1))
                                elif not first_a:
                                    act.wait_ge(s_abs, at(ta - 1, 2 * HEADS, 2 * HEADS + k - 1))
                                act.activation(junk[:, n, :], prob[:, g % 2, h % 2, n, :], ACT.Abs,
                                               accum_out=asum[:, h, n:n + 1]).then_inc(s_abs, 1)
                            for n in range(NT):
                                p = prob[:, g % 2, h % 2, n, :]
                                act.wait_ge(s_abs, at(ta, 2 * HEADS, 2 * h + n + 1))
                                act.activation(p, p, ACT.Exp, bias=nmax[:, h, n:n + 1], scale=-1.0,
                                               accum_out=esum[:, h, n:n + 1]).then_inc(s_exp, 1)
                    if name == "T":
                        g, = arg
                        if g > 0:
                            act.wait_ge(pv_used, at(ta, PAIRS, g))
                        else:
                            for k in range(2, PAIRS):
                                act.wait_ge(stacked[k], at(ta, 16 * 6, 16 * 6))
                        for i in range(2):
                            act.wait_ge(pt_full, at(ta, HEADS, 2 * g + i + 1))
                            act.activation(pt_hi[:, 2 * i:2 * i + 2, :],
                                           bank[2 + i][:, :].rearrange("p (k n) -> p k n", k=NT),
                                           ACT.Copy).then_inc(pt_hi_s, 1)
                    if name == "PV" and arg[0] % 2 == 1:
                        c = arg[0] // 2
                        act.wait_ge(pv_used, at(ta, PAIRS, arg[0] + 1))
                        if c == 0:
                            act.wait_ge(v_full, at(ta, NT, NT))
                        act.activation(xo_hi[:, c, :], ov_bank[:, 0:N], ACT.Copy).then_inc(ot_hi, 1)
                    if name == "AT":
                        act.wait_ge(at_full, at(ta, 1, 1))
                        if not first_a:
                            act.wait_ge(u_adj, at(ta - 1, 4, 4))
                        act.activation(adjT[:, :, :], bank[2][:, :].rearrange("p (k n) -> p k n", k=NT),
                                       ACT.Copy).then_inc(at_done, 1)
                    if name == "ht":
                        l, = arg
                        for u, w in enumerate((2, 1)):
                            act.wait_ge(t_full, at(tb, 4, 2 * l + u + 1))
                            b = b_bank(l, f"T{u}")
                            if l == 0:
                                if u == 0 and not first_b:
                                    act.wait_ge(u_full, at(tb - 1, 4, 4))
                                    act.wait_ge(l_full, at(tb - 1, 4, 4))
                                act.activation(h_hi[:, 2 * u:2 * u + w, :],
                                               b[:, 0:w * N].rearrange("p (c n) -> p c n", c=w),
                                               ACT.Copy).then_inc(h_hi_s, 1)
                            else:
                                for c in range(2 * u, 2 * u + w):
                                    if c == 0:
                                        act.wait_ge(s_col, 64)
                                        act.wait_ge(u_exp, at(tb, 4, 2))
                                    act.activation(hT[:, c, :], b[:, (c % 2) * N:(c % 2 + 1) * N], ACT.Relu,
                                                   scale=a_col[:, c:c + 1],
                                                   bias=b_col[:, c:c + 1]).then_inc(h_f32, 1)
                                act.wait_ge(h_f32, at(tb, HC, 2 * u + w))
                                if u == 0:
                                    act.wait_ge(u_full, at(tb, 4, 2))
                                    act.wait_ge(l_full, at(tb, 4, 2))
                                act.activation(h_hi[:, 2 * u:2 * u + w, :], hT[:, 2 * u:2 * u + w, :],
                                               ACT.Copy).then_inc(h_hi_s, 1)
                    if name == "m":
                        l, u = arg
                        act.wait_ge(m_full, at(tb, 6, 3 * l + u + 1))
                        if u == 0 and (l > 0 or not first_b):
                            act.wait_ge(c_full, at(tb, 4, 2) if l > 0 else at(tb - 1, 4, 4))
                        act.activation(m_hi[:, 2 * u:2 * u + 2, :],
                                       b_bank(l, f"M{u}")[:, :].rearrange("p (c n) -> p c n", c=2),
                                       ACT.Copy).then_inc(m_hi_s, 1)
                    if name == "lin":
                        l, = arg
                        if l > 0 or not first_b:
                            act.wait_ge(c_full, at(tb, 4, 2) if l > 0 else at(tb - 1, 4, 4))
                        for n in range(NT):
                            act.wait_ge(l_full, at(tb, 4, 2 * l + n + 1))
                            act.activation(l_hi[:, n, 0:H], b_bank(l, f"L{n}")[:, 0:H],
                                           ACT.Copy).then_inc(l_hi_s, 1)
                    if name == "u":
                        l, = arg
                        for J in range(NT):
                            act.wait_ge(u_add, at(tb, 4, 2 * l + J + 1))
                            if J == 0 and (l > 0 or not first_b):
                                act.wait_ge(e_lo_s, at(tb, 4, 2) if l > 0 else at(tb - 1, 4, 4))
                            act.activation(ex[:, J, :], um[:, J, (1 - J) * P:(1 - J) * P + N], ACT.Exp,
                                           scale=SCALE).then_inc(u_exp, 1)
                    if name == "e":
                        l, = arg
                        act.wait_ge(u_full, at(tb, 4, 2 * l + 2))
                        for J in range(NT):
                            act.wait_ge(u_adj, at(tb, 4, 2 * l + J + 1))
                            act.activation(e_hi[:, J, :], ex[:, J, :], ACT.Copy).then_inc(e_hi_s, 1)
                    if name in ("z", "zc"):
                        t, l = (tb, 0) if name == "z" else (tc, 1)
                        if l == 0 and not first_b:
                            act.wait_ge(stored, at(tb - 1, 16, 16))
                        if l == 1:
                            act.wait_ge(t_full, at(tc, 4, 4))
                        act.wait_ge(b_off, at(t, 2, l + 1))
                        for n in range(NT):
                            act.activation(cz[:, n, :], b_bank(l, f"C{n}")[:, 0:H], ACT.Identity,
                                           scale=zfac[:, n:n + 1], bias=zoff[:, n:n + 1]).then_inc(z_ready, 1)

            turns(act, body)

        @block.vector
        def _(dve):
            def factors(t, l, first):
                dve.wait_ge(b_std, at(t, 2, l + 1))
                dve.scalar_tensor_tensor(out=sden[:, :], in0=std_b[:, :], scalar=(H / (H - 1.0)) ** 0.5,
                                         in1=den[:, :], op0=ALU.mult, op1=ALU.add).then_inc(b_stde, 1)
                if l == 1:
                    dve.wait_ge(z_ready, at(t, 4, 2))
                elif not first:
                    dve.wait_ge(z_ready, at(t - 1, 4, 4))
                dve.wait_ge(b_stde, at(t, 2, l + 1))
                dve.reciprocal(zfac[:, :], sden[:, :]).then_inc(b_fac, 1)
                dve.wait_ge(b_fac, at(t, 2, l + 1))
                dve.scalar_tensor_tensor(out=zoff[:, :], in0=stat_b[:, :, 6], scalar=-1.0, in1=zfac[:, :],
                                         op0=ALU.mult, op1=ALU.mult).then_inc(b_off, 1)

            dve.memset(r32(stack[SR:P, 1, 0, 0:P]), 1.0).then_inc(s_zero, 1)
            dve.wait_ge(s_bias, 16 * len(BIAS))
            for n in range(len(BIAS)):
                dve.tensor_copy(bias_hi[n], bias_raw[n]).then_inc(s_bhi, 1)
            dve.wait_ge(s_bhi, len(BIAS))
            for n in range(len(BIAS)):
                dve.tensor_tensor(bias_lo[n], bias_raw[n], r32(bias_hi[n]), ALU.subtract).then_inc(s_blo, 1)
            def slice_lo(i):
                dst = slice(i % HC * P, (i % HC + 1) * P)
                dve.wait_ge(s_whi, i + 1)
                dve.scalar_tensor_tensor(out=w_lo[:, i // HC, :, dst],
                                         in0=w_bank(i)[:, 0:H].rearrange("p (c o) -> p c o", c=HC),
                                         scalar=0.5 * SCALE if i // HC == Q_ else 1.0,
                                         in1=r32(w_hi[:, i // HC, :, dst]),
                                         op0=ALU.mult, op1=ALU.subtract).then_inc(s_wlo, 1)

            for i in range(EARLY):
                slice_lo(i)

            def body(ta, tb, tc, first_a, first_b, more):
                for name, arg in steps("dve", ta, tb, tc):
                    if name == "W":
                        slice_lo(arg[0])
                    if name == "XT":
                        for u, w in enumerate((2, 1)):
                            dve.wait_ge(xt_hi, at(ta, 2, u + 1))
                            dve.tensor_tensor(xo_lo[:, 2 * u:2 * u + w, :],
                                              bank[u][:, 0:w * N].rearrange("p (c n) -> p c n", c=w),
                                              r32(xo_hi[:, 2 * u:2 * u + w, :]), ALU.subtract).then_inc(xt_lo, 1)
                    if name == "QK":
                        m, = arg
                        dve.wait_ge(qk_hi, at(ta, HC, m + 1))
                        dve.tensor_tensor(qk_part[:, m % 2, 1:4:2, :],
                                          bank[2 + m][:, :].rearrange("p (a n) -> p a n", a=2),
                                          r32(qk_part[:, m % 2, 0:3:2, :]), ALU.subtract).then_inc(qk_lo, 1)
                    if name == "V":
                        for n in range(NT):
                            dve.wait_ge(v_hi_s, at(ta, 2 * NT, 2 * n + 2))
                            for a in range(2):
                                dve.tensor_tensor(v_view(v_lo, n, a), v_src(n, a), r32(v_view(v_hi, n, a)),
                                                  ALU.subtract).then_inc(v_lo_s, 1)
                    if name == "S":
                        g, = arg
                        if g == 0:
                            dve.wait_ge(adj_ld, at(ta, 16, 16))
                            if not first_a:
                                dve.wait_ge(pt_full, at(ta - 1, HEADS, HEADS))
                        elif g >= 2:
                            dve.wait_ge(pt_full, at(ta, HEADS, 2 * g - 2))
                        for i in range(2):
                            h = 2 * g + i
                            wait_apart(dve, s_full, at(ta, HEADS, h + 1))
                            for n in range(NT):
                                dve.tensor_tensor_reduce(prob[:, g % 2, i, n, :], bank[h % 2][:, n * N:(n + 1) * N],
                                                         adj_in[:, n, :], -2.0, 3.0e38, ALU.add, ALU.min,
                                                         nmax[:, h, n:n + 1]).then_inc(s_neg, 1)
                    if name == "N":
                        g, = arg
                        hs = slice(2 * g, 2 * g + 2)
                        dve.wait_ge(s_exp, at(ta, 2 * HEADS, 4 * g + 4))
                        dve.reciprocal(rsum[:, hs, :], esum[:, hs, :]).then_inc(s_rec, 1)
                        dve.wait_ge(s_rec, at(ta, PAIRS, g + 1))
                        dve.scalar_tensor_tensor(out=rsum[:, hs, :], in0=asum[:, hs, :], scalar=0.0,
                                                 in1=rsum[:, hs, :], op0=ALU.not_equal,
                                                 op1=ALU.mult).then_inc(s_rn, 1)
                        dve.wait_ge(s_rn, at(ta, PAIRS, g + 1))
                        for i in range(2):
                            for n in range(NT):
                                p = prob[:, g % 2, i, n, :]
                                ins = dve.tensor_scalar(p, p, rsum[:, 2 * g + i, n:n + 1], None, ALU.mult)
                            ins.then_inc(s_norm, 1)
                    if name == "T":
                        g, = arg
                        for i in range(2):
                            dve.wait_ge(pt_hi_s, at(ta, HEADS, 2 * g + i + 1))
                            dve.tensor_tensor(pt_lo[:, 2 * i:2 * i + 2, :],
                                              bank[2 + i][:, :].rearrange("p (k n) -> p k n", k=NT),
                                              r32(pt_hi[:, 2 * i:2 * i + 2, :]), ALU.subtract).then_inc(pt_lo_s, 1)
                    if name == "PV" and arg[0] % 2 == 1:
                        c = arg[0] // 2
                        dve.wait_ge(ot_hi, at(ta, HC, c + 1))
                        dve.tensor_tensor(xo_lo[:, c, :], ov_bank[:, 0:N], r32(xo_hi[:, c, :]),
                                          ALU.subtract).then_inc(ot_lo, 1)
                    if name == "O":
                        dve.wait_ge(x_res, at(ta, 16, 16))
                        for n in range(NT):
                            dve.wait_ge(o_full, at(ta, NT, n + 1))
                            dve.tensor_tensor(x1[:, n, :], bank[n][:, 0:H], x1[:, n, :], ALU.add).then_inc(o_sum, 1)
                            dve.wait_ge(o_sum, at(ta, NT, n + 1))
                            dve.bn_stats(stat_a[:, n, 0:6], x1[:, n, :]).then_inc(a_stat, 1)
                        wait_apart(dve, a_stat, at(ta, NT, NT))
                        for n in range(NT):
                            dve.bn_aggr(stat_a[:, n, 6:8], stat_a[:, n, 0:6]).then_inc(a_aggr, 1)
                        dve.wait_ge(a_aggr, at(ta, NT, NT))
                        dve.tensor_scalar(rstd_a[:, :], stat_a[:, :, 7], LN_EPS, None,
                                          ALU.add).then_inc(a_var, 1)
                    if name == "LN":
                        dve.wait_ge(a_rstd, at(ta, 1, 1))
                        for n in range(NT):
                            dve.tensor_scalar(x1[:, n, :], x1[:, n, :], stat_a[:, n, 6:7], rstd_a[:, n:n + 1],
                                              ALU.subtract, ALU.mult).then_inc(x1_ready, 1)
                    if name == "ht":
                        l, = arg
                        for u, w in enumerate((2, 1)):
                            hs = slice(2 * u, 2 * u + w)
                            dve.wait_ge(h_hi_s, at(tb, 4, 2 * l + u + 1))
                            src = b_bank(l, f"T{u}")[:, 0:w * N].rearrange("p (c n) -> p c n", c=w)
                            dve.tensor_tensor(h_lo[:, hs, :], src if l == 0 else hT[:, hs, :],
                                              r32(h_hi[:, hs, :]), ALU.subtract).then_inc(h_lo_s, 1)
                    if name == "m":
                        l, u = arg
                        dve.wait_ge(m_hi_s, at(tb, 6, 3 * l + u + 1))
                        dve.tensor_tensor(m_lo[:, 2 * u:2 * u + 2, :],
                                          b_bank(l, f"M{u}")[:, :].rearrange("p (c n) -> p c n", c=2),
                                          r32(m_hi[:, 2 * u:2 * u + 2, :]), ALU.subtract).then_inc(m_lo_s, 1)
                    if name == "lin":
                        l, = arg
                        for n in range(NT):
                            dve.wait_ge(l_hi_s, at(tb, 4, 2 * l + n + 1))
                            dve.tensor_tensor(l_lo[:, n, 0:H], b_bank(l, f"L{n}")[:, 0:H], r32(l_hi[:, n, 0:H]),
                                              ALU.subtract).then_inc(l_lo_s, 1)
                    if name == "u":
                        l, = arg
                        if l == 0:
                            dve.wait_ge(masks, at(tb, 1, 1))
                            if not first_b:
                                dve.wait_ge(u_exp, at(tb - 1, 4, 4))
                        else:
                            dve.wait_ge(h_lo_s, at(tb, 4, 4))
                        for J in range(NT):
                            dve.wait_ge(u_full, at(tb, 4, 2 * l + J + 1))
                            dve.tensor_tensor(um[:, J, :], b_bank(l, f"U{J}")[:, 0:3 * P], mask[:, J, :],
                                              ALU.mult).then_inc(u_mask, 1)
                        for J in range(NT):
                            dve.wait_ge(u_mask, at(tb, 4, 2 * l + J + 1))
                            o = 2 * J * P
                            dve.tensor_tensor(um[:, J, P:2 * P], um[:, J, P:2 * P], um[:, J, o:o + P],
                                              ALU.add).then_inc(u_add, 1)
                    if name == "e":
                        l, = arg
                        for J in range(NT):
                            dve.wait_ge(e_hi_s, at(tb, 4, 2 * l + J + 1))
                            dve.tensor_tensor(e_lo[:, J, :], ex[:, J, :], r32(e_hi[:, J, :]),
                                              ALU.subtract).then_inc(e_lo_s, 1)
                    if name == "ctx":
                        l, = arg
                        if l > 0 or not first_b:
                            wait_apart(dve, b_off, at(tb, 2, 1) if l > 0 else at(tb - 1, 2, 2))
                        for n in range(NT):
                            wait_apart(dve, c_full, at(tb, 4, 2 * l + n + 1))
                            dve.tensor_scalar(den[:, n:n + 1], b_bank(l, f"C{n}")[:, H:H + 1], SUM_EPS, STD_EPS,
                                              ALU.add, ALU.mult).then_inc(c_den, 1)
                            dve.bn_stats(stat_b[:, n, 0:6], b_bank(l, f"C{n}")[:, 0:H]).then_inc(b_stat, 1)
                        wait_apart(dve, b_stat, at(tb, 4, 2 * l + 2))
                        for n in range(NT):
                            dve.bn_aggr(stat_b[:, n, 6:8], stat_b[:, n, 0:6]).then_inc(b_aggr, 1)
                    if name == "z":
                        wait_apart(dve, c_den, at(tb, 4, 2))
                        factors(tb, 0, first_b)
                    if name == "zc":
                        wait_apart(dve, c_den, at(tc, 4, 4))
                        factors(tc, 1, False)
                    if name == "residual":
                        dve.wait_ge(res_kept, at(tc, 1, 1))
                        for n in range(NT):
                            dve.wait_ge(f_add, at(tc, NT, n + 1))
                            dve.scalar_tensor_tensor(out=cz[:, n, :], in0=cz[:, n, :], scalar=0.0,
                                                     in1=x1_res[:, n, :], op0=ALU.max,
                                                     op1=ALU.add).then_inc(f_res, 1)
                        for n in range(NT):
                            dve.wait_ge(f_res, at(tc, NT, n + 1))
                            dve.bn_stats(stat_f[:, n, 0:6], cz[:, n, :]).then_inc(f_stat, 1)
                        wait_apart(dve, f_stat, at(tc, NT, NT))
                        for n in range(NT):
                            dve.bn_aggr(stat_f[:, n, 6:8], stat_f[:, n, 0:6]).then_inc(f_aggr, 1)
                        dve.wait_ge(f_aggr, at(tc, NT, NT))
                        dve.tensor_scalar(rstd_f[:, :], stat_f[:, :, 7], LN_EPS, None,
                                          ALU.add).then_inc(f_var, 1)
                    if name == "store":
                        dve.wait_ge(f_rstd, at(tc, 1, 1))
                        for n in range(NT):
                            dve.tensor_scalar(cz[:, n, :], cz[:, n, :], stat_f[:, n, 6:7], rstd_f[:, n:n + 1],
                                              ALU.subtract, ALU.mult).then_inc(f_out, 1)

            turns(dve, body)

        @block.gpsimd
        def _(pool):
            pool.memset(ident[:, :], 0.0).then_inc(s_id, 1)
            pool.wait_ge(s_id, 1)
            pool.affine_select(out=ident[:, :], in_=ident[:, :], compare_op=ALU.not_equal, fill=1.0, base=0,
                               pattern=[[-1, P]], channel_multiplier=1).then_inc(s_id, 1)
            pool.memset(power[:, 0, :], -0.5).then_inc(s_pow, 1)
            pool.memset(power[:, 1, :], 0.5).then_inc(s_pow, 1)
            pool.wait_ge(s_pow, 2)
            pool.memset(r32(v_hi[:, :, :, :]), 0.0).then_inc(s_zero, 1)
            pool.memset(r32(v_lo[:, :, :, :]), 0.0).then_inc(s_zero, 1)
            pool.memset(r32(l_hi[:, :, H:H + 2]), 1.0).then_inc(s_zero, 1)
            pool.memset(r32(l_lo[:, :, H:H + 2]), 0.0).then_inc(s_zero, 1)
            pool.wait_ge(s_col, 64)

            def body(ta, tb, tc, first_a, first_b, more):
                for name, arg in steps("pool", ta, tb, tc):
                    if name == "AT":
                        pool.wait_ge(at_done, at(ta, 1, 1))
                        if not first_a:
                            wait_apart(pool, u_mask, at(ta - 1, 4, 4))
                        for o, src, cm, st, base, w in (
                                (mask[:, 0, 0:P], adjT[:, 0, 0:P], 1, -1, 0, P),
                                (mask[:, 0, P:3 * P], adj_in[:, 0, :], -1, 1, -1, N),
                                (mask[:, 1, 0:2 * P], adjT[:, 1, :], 1, -1, P, N),
                                (mask[:, 1, 2 * P:3 * P], adj_in[:, 1, P:N], -1, 1, -1, P)):
                            ins = pool.affine_select(out=o, in_=src, compare_op=ALU.is_ge, fill=0.0, base=base,
                                                     pattern=[[st, w]], channel_multiplier=cm)
                        ins.then_inc(masks, 1)
                    if name == "O":
                        pool.wait_ge(a_var, at(ta, 1, 1))
                        pool.tensor_tensor(rstd_a[:, :], rstd_a[:, :], power[:, 0, :], ALU.pow).then_inc(a_rstd, 1)
                    if name == "ctx":
                        pool.wait_ge(b_aggr, at(tb, 4, 2 * arg[0] + 2))
                        pool.tensor_tensor(std_b[:, :], stat_b[:, :, 7], power[:, 1, :], ALU.pow).then_inc(b_std, 1)
                    if name == "keep":
                        pool.wait_ge(t_full, at(tb, 4, 2))
                        if not first_b:
                            wait_apart(pool, f_res, at(tb - 1, NT, NT))
                        pool.tensor_copy(x1_res[:, :, :], x1[:, :, :]).then_inc(res_kept, 1)
                    if name == "e":
                        l, = arg
                        for J in range(NT):
                            pool.wait_ge(u_exp, at(tb, 4, 2 * l + J + 1))
                            pool.tensor_tensor(ex[:, J, :], ex[:, J, :], adjT[:, J, :], ALU.mult).then_inc(u_adj, 1)
                    if name == "affine":
                        for n in range(NT):
                            pool.wait_ge(z_ready, at(tc, 4, 2 + n + 1))
                            pool.tensor_tensor(cz[:, n, :], cz[:, n, :], a_row[:, :], ALU.mult).then_inc(f_mul, 1)
                            pool.wait_ge(f_mul, at(tc, NT, n + 1))
                            pool.tensor_tensor(cz[:, n, :], cz[:, n, :], b_row[:, :], ALU.add).then_inc(f_add, 1)
                    if name == "residual":
                        pool.wait_ge(f_var, at(tc, 1, 1))
                        pool.tensor_tensor(rstd_f[:, :], rstd_f[:, :], power[:, 0, :], ALU.pow).then_inc(f_rstd, 1)

            turns(pool, body)


_INS = ["x", "adj", "L0_gnn_Wq", "L0_gnn_Wk", "L0_gnn_Wv", "L0_gnn_bv", "L0_gnn_Wo", "L0_gnn_bo",
        "L1_gnn_W_left", "L1_gnn_W_right", "L1_gnn_W_lin", "L1_gnn_b_lin", "L1_gnn_ln_a", "L1_gnn_ln_b"]
_OUTS = [((32, 256, 384), "float32")]


def kernel(**inputs):
    import numpy as _np
    import concourse.bacc as _bacc
    from concourse import mybir as _mybir
    from concourse.bass_utils import run_bass_kernel_spmd as _run

    nc = _bacc.Bacc("TRN2", target_bir_lowering=False, num_devices=1)
    arrays, args = {}, []
    for name in _INS:
        a = _np.ascontiguousarray(inputs[name])
        arrays[f"in_{name}_dram"] = a
        args.append(nc.dram_tensor(f"in_{name}_dram", a.shape, _mybir.dt.from_np(a.dtype), kind="ExternalInput").ap())
    for i, (shape, dtype) in enumerate(_OUTS):
        dt = _mybir.dt.from_np(_np.dtype(dtype))
        args.append(nc.dram_tensor(f"out_{i}_dram", shape, dt, kind="ExternalOutput").ap())
    adj_resnorm_kernel(nc, *args)
    r = _run(nc, [arrays], core_ids=[0])
    got = tuple(r.results[0][f"out_{i}_dram"] for i in range(len(_OUTS)))
    return got[0]
```
